# Optimizing a Trainium2 kernel written in Bass

```python
import numpy as np
import jax
import jax.numpy as jnp

def _softmax(x, axis=-1):
    return jax.nn.softmax(x, axis=axis)

def _gelu(x):
    return jax.nn.gelu(x, approximate=True)

def _silu(x):
    return jax.nn.silu(x)

def _sigmoid(x):
    return jax.nn.sigmoid(x)

def _layernorm(x, axis=-1, eps=1e-05):
    m = jnp.mean(x, axis=axis, keepdims=True)
    v = jnp.var(x, axis=axis, keepdims=True)
    return (x - m) / jnp.sqrt(v + eps)

def _scatter_add(tgt, idx, src, axis=0):
    return tgt.at[idx].add(src)

def _segment_sum(src, seg, n):
    return jax.ops.segment_sum(src, seg, n)
kernel_name = 'mk_vit_tower_d1_tok_img768_r4_33c351'

def setup_inputs(seed: int=0):
    np.random.seed(seed)
    _w = jnp.asarray

    def _rec_inputs():
        import jax
        import jax.numpy as jnp
        _rk = jax.random.key(seed)
        x = -0.00016672 + 0.999947 * jax.random.normal(jax.random.fold_in(_rk, 1), (16, 3, 96, 96), jnp.float32)
        return x
    x = _rec_inputs()

    def _L0_tok_setup():
        import jax, jax.numpy as jnp
        import numpy as np
        EPS = 0.0001
        P = 16

        def rms_norm(x, g, eps=EPS):
            ms = jnp.mean(jnp.square(x), axis=-1, keepdims=True)
            return x * jax.lax.rsqrt(ms + eps) * g
        key = jax.random.key(seed)
        k1, k2, k3 = jax.random.split(key, 3)
        B, C, H, W = (64, 3, 96, 96)
        patch_dim = C * P * P
        proj_dim = 192
        x = jax.random.normal(k1, (B, C, H, W), dtype=jnp.float32)
        g1 = jnp.ones((patch_dim,), dtype=jnp.float32)
        Wp = jax.random.normal(k2, (patch_dim, proj_dim), dtype=jnp.float32) / np.sqrt(patch_dim)
        bp = jax.random.normal(k3, (proj_dim,), dtype=jnp.float32) * 0.01
        g2 = jnp.ones((proj_dim,), dtype=jnp.float32)
        return {'x': x, 'g1': g1, 'Wp': Wp, 'bp': bp, 'g2': g2}
    _L0_tok_all = _L0_tok_setup()
    _L0_tok_in = {k: v for k, v in _L0_tok_all.items() if k in ('g1', 'Wp', 'bp', 'g2')}
    del _L0_tok_all

    def _L0_attn_setup():
        import jax, jax.numpy as jnp
        import numpy as np
        N_HEADS = 12
        key = jax.random.key(seed)
        k1, k2, k3 = jax.random.split(key, 3)
        B, S, W = (8, 256, 192)
        x = jax.random.normal(k1, (B, S, W), dtype=jnp.float32)
        w_qkv = jax.random.normal(k2, (W, 3 * W), dtype=jnp.float32) * W ** (-0.5)
        w_out = jax.random.normal(k3, (W, W), dtype=jnp.float32) * W ** (-0.5)
        return {'x': x, 'w_qkv': w_qkv, 'w_out': w_out}
    _L0_attn_all = _L0_attn_setup()
    _L0_attn_in = {k: v for k, v in _L0_attn_all.items() if k in ('w_qkv', 'w_out')}
    del _L0_attn_all

    def _L0_ffn_setup():
        import jax, jax.numpy as jnp
        import numpy as np
        GT0 = [[0, 1, 0, 0, 1, 0], [0, 1, 0, 0, 0, 1], [0, 0, 1, 0, 1, 0], [0, 0, 1, 0, 0, 1], [0, 0, 0, 1, 1, 0], [0, 0, 0, 1, 0, 1]]
        NCLS = 6
        K = 1

        def _expert_pairs():
            pairs = []
            for i in range(NCLS):
                p = [(j - 1, k - 1) for j in range(1, 6) for k in range(1, 6) if j != k and GT0[i][j] == 1 and (GT0[i][k] == 1)]
                pairs.append(p)
            return pairs
        PAIRS = _expert_pairs()
        B, P, D, H = (64, 64, 192, 768)

        def _gelu(t):
            return jax.nn.gelu(t, approximate=False)
        key = jax.random.key(seed)
        ks = jax.random.split(key, 8)
        s = 0.02
        x = jax.random.normal(ks[0], (B, NCLS + P, D), dtype=jnp.float32)
        mids = jax.random.randint(ks[1], (B,), 0, 6)
        moe0_W1 = jax.random.normal(ks[2], (D, H), dtype=jnp.float32) * s
        moe0_b1 = jnp.zeros((H,), jnp.float32)
        moe0_W2 = jax.random.normal(ks[3], (H, D), dtype=jnp.float32) * s
        moe0_b2 = jnp.zeros((D,), jnp.float32)
        A1_W = jax.random.normal(ks[4], (5, D, H), dtype=jnp.float32) * s
        A1_b = jnp.zeros((5, H), jnp.float32)
        A2_W = jax.random.normal(ks[5], (5, H, D), dtype=jnp.float32) * s
        A2_b = jnp.zeros((5, D), jnp.float32)
        G_W = jax.random.normal(ks[6], (NCLS, D, 2), dtype=jnp.float32) * s
        return {'x': x, 'moe0_W1': moe0_W1, 'moe0_b1': moe0_b1, 'moe0_W2': moe0_W2, 'moe0_b2': moe0_b2, 'A1_W': A1_W, 'A1_b': A1_b, 'A2_W': A2_W, 'A2_b': A2_b, 'G_W': G_W, 'mids': mids}
    _L0_ffn_all = _L0_ffn_setup()
    _L0_ffn_in = {k: v for k, v in _L0_ffn_all.items() if k in ('moe0_W1', 'moe0_b1', 'moe0_W2', 'moe0_b2', 'A1_W', 'A1_b', 'A2_W', 'A2_b', 'G_W', 'mids')}
    del _L0_ffn_all
    return {'x': x, 'L0_tok_g1': _L0_tok_in['g1'], 'L0_tok_Wp': _L0_tok_in['Wp'], 'L0_tok_bp': _L0_tok_in['bp'], 'L0_tok_g2': _L0_tok_in['g2'], 'L0_attn_w_qkv': _L0_attn_in['w_qkv'], 'L0_attn_w_out': _L0_attn_in['w_out'], 'L0_ffn_moe0_W1': _L0_ffn_in['moe0_W1'], 'L0_ffn_moe0_b1': _L0_ffn_in['moe0_b1'], 'L0_ffn_moe0_W2': _L0_ffn_in['moe0_W2'], 'L0_ffn_moe0_b2': _L0_ffn_in['moe0_b2'], 'L0_ffn_A1_W': _L0_ffn_in['A1_W'], 'L0_ffn_A1_b': _L0_ffn_in['A1_b'], 'L0_ffn_A2_W': _L0_ffn_in['A2_W'], 'L0_ffn_A2_b': _L0_ffn_in['A2_b'], 'L0_ffn_G_W': _L0_ffn_in['G_W'], 'L0_ffn_mids': _L0_ffn_in['mids']}

def reference(x, L0_tok_g1, L0_tok_Wp, L0_tok_bp, L0_tok_g2, L0_attn_w_qkv, L0_attn_w_out, L0_ffn_moe0_W1, L0_ffn_moe0_b1, L0_ffn_moe0_W2, L0_ffn_moe0_b2, L0_ffn_A1_W, L0_ffn_A1_b, L0_ffn_A2_W, L0_ffn_A2_b, L0_ffn_G_W, L0_ffn_mids):
    import jax
    import jax.numpy as jnp

    def _L0_tok_ref(x, g1, Wp, bp, g2):
        import jax, jax.numpy as jnp
        import numpy as np
        EPS = 0.0001
        P = 16

        def rms_norm(x, g, eps=EPS):
            ms = jnp.mean(jnp.square(x), axis=-1, keepdims=True)
            return x * jax.lax.rsqrt(ms + eps) * g
        B, C, H, W = x.shape
        h, w = (H // P, W // P)
        patches = x.reshape(B, C, h, P, w, P)
        patches = patches.transpose(0, 2, 4, 3, 5, 1)
        patches = patches.reshape(B, h * w, P * P * C)
        y = rms_norm(patches, g1)
        y = jnp.einsum('bnd,de->bne', y, Wp) + bp
        return rms_norm(y, g2)

    def _L0_attn_ref(x, w_qkv, w_out):
        import jax, jax.numpy as jnp
        import numpy as np
        N_HEADS = 12
        B, S, W = x.shape
        H = N_HEADS
        D = W // H
        scale = W ** (-0.5)
        qkv = x @ w_qkv
        q, k, v = jnp.split(qkv, 3, axis=2)
        q = q.reshape(B, S, H, D)
        k = k.reshape(B, S, H, D)
        attn_score = jnp.einsum('binh,bjnh->bijn', q, k) * scale
        attn_weight = jax.nn.softmax(attn_score, axis=2)
        out = jnp.einsum('bijn,bjnh->binh', attn_weight, k)
        out = out.reshape(B, S, W)
        return out @ w_out

    def _L0_ffn_ref(x, moe0_W1, moe0_b1, moe0_W2, moe0_b2, A1_W, A1_b, A2_W, A2_b, G_W, mids):
        import jax, jax.numpy as jnp
        import numpy as np
        GT0 = [[0, 1, 0, 0, 1, 0], [0, 1, 0, 0, 0, 1], [0, 0, 1, 0, 1, 0], [0, 0, 1, 0, 0, 1], [0, 0, 0, 1, 1, 0], [0, 0, 0, 1, 0, 1]]
        NCLS = 6
        K = 1

        def _expert_pairs():
            pairs = []
            for i in range(NCLS):
                p = [(j - 1, k - 1) for j in range(1, 6) for k in range(1, 6) if j != k and GT0[i][j] == 1 and (GT0[i][k] == 1)]
                pairs.append(p)
            return pairs
        PAIRS = _expert_pairs()
        B, P, D, H = (64, 64, 192, 768)

        def _gelu(t):
            return jax.nn.gelu(t, approximate=False)
        cls_tokens = x[:, :NCLS]
        patch_tokens = x[:, NCLS:]
        patch_out = _gelu(patch_tokens @ moe0_W1 + moe0_b1) @ moe0_W2 + moe0_b2
        cls_outs = []
        for i in range(NCLS):
            tok = cls_tokens[:, i]
            eouts = [_gelu(tok @ A1_W[a] + A1_b[a]) @ A2_W[c] + A2_b[c] for a, c in PAIRS[i]]
            out = jnp.stack(eouts, axis=-1)
            gate = jax.nn.softmax(tok @ G_W[i], axis=-1)
            thr = jnp.sort(gate, axis=-1)[..., -(K + 1)]
            mask = (gate > thr[..., None]).astype(gate.dtype)
            g = gate * mask
            g = g / jnp.clip(jnp.sum(g, axis=-1, keepdims=True), 1e-06)
            cls_outs.append(jnp.sum(out * g[:, None, :], axis=-1))
        cls_out = jnp.stack(cls_outs, axis=1)
        return jnp.concatenate([cls_out, patch_out], axis=1)
    h = _L0_tok_ref(x, L0_tok_g1, L0_tok_Wp, L0_tok_bp, L0_tok_g2)
    h = h + _L0_attn_ref(_layernorm(h, axis=-1), L0_attn_w_qkv, L0_attn_w_out)
    h = h + _L0_ffn_ref(_layernorm(h, axis=-1), L0_ffn_moe0_W1, L0_ffn_moe0_b1, L0_ffn_moe0_W2, L0_ffn_moe0_b2, L0_ffn_A1_W, L0_ffn_A1_b, L0_ffn_A2_W, L0_ffn_A2_b, L0_ffn_G_W, L0_ffn_mids)
    return h

_drawn_inputs = setup_inputs


def setup_inputs(seed=0):
    import zlib

    import numpy as np

    out = dict(_drawn_inputs(seed))
    spreads = {'L0_tok_g1': (1.0, 0.2),
     'L0_tok_g2': (1.0, 0.2),
     'L0_ffn_moe0_b1': (0.0, 0.32),
     'L0_ffn_moe0_b2': (0.0, 0.1),
     'L0_ffn_A1_b': (0.0, 0.713),
     'L0_ffn_A2_b': (0.0, 0.1)}
    factors = {'L0_tok_bp': 3.998}
    for name, (base, spread) in spreads.items():
        noise = np.random.default_rng([zlib.crc32(name.encode()), seed]).standard_normal(out[name].shape)
        drawn = base * np.exp(spread * noise) if base else spread * noise
        out[name] = jnp.asarray(drawn.astype(out[name].dtype))
    for name, factor in factors.items():
        out[name] = (out[name] * factor).astype(out[name].dtype)
    return out
```

```python
from contextlib import ExitStack

import concourse.bass as bass
from concourse import mybir

F32 = mybir.dt.float32
ALU = mybir.AluOpType
ACT = mybir.ActivationFunctionType
AX = mybir.AxisListType

B, C, IMG, PATCH = 16, 3, 96, 16
G = IMG // PATCH
N = G * G
T = G * B
NTOK = B * N
PD = C * PATCH * PATCH
KT = PD // 128
E = 192
EH = E // 2
HEADS, D = 12, 16
SLOTS = 3
HALF = SLOTS * D
HPAD = 64
QR = HPAD + HALF
SP = SLOTS * N
SC = 2 * N
PR = HPAD + N
F = 768
M = F // 128
NE = 5
NCLS = 6
UNIT = 2
NU = B // UNIT
CHUNK = 8
EPS_RMS, EPS_LN = 1e-4, 1e-5
EXPERT_COLS = [0, 32, 64, 96, 144]
EXPERT_TOK = [32, 32, 32, 48, 48]
HT = 192
PAIRS = G // 2

XT_BANK, EMB_BANK, R1_BANK = (0, 1), (2, 3, 4, 5, 6, 7), 0
LN1_BANK, QK_BANK = (0, 1), (2, 3, 4, 5, 6, 7)
S_BANK, PV_BANK, KP_BANK, PT_BANK = (0, 1), (2, 3), (4, 5), (6, 7)
WO_BANK, LN2_BANK, GATE_BANK, A1_BANK = (0, 1, 4, 5), (6, 7), 2, (3, 2)
GB_BANK, F1_BANK, A2_BANK, F2_BANK, CLS_BANK = 1, (4, 5), 0, (2, 3), 6


def vit_tower(nc: bass.Bass, x, g1, wp, bp, g2, w_qkv, w_out, moe_w1, moe_b1, moe_w2, moe_b2,
              a1_w, a1_b, a2_w, a2_b, g_w, out):
    with ExitStack() as ctx:
        def sb(name, shape):
            return ctx.enter_context(nc.sbuf_tensor(name, shape, F32))

        def sem(name):
            return ctx.enter_context(nc.semaphore(name))

        bank = [ctx.enter_context(nc.psum_tensor(f"bank{i}", [128, 512], F32)) for i in range(8)]

        wp_g = sb("wp_g", [128, KT, E])
        g1_sb = sb("g1_sb", [128, KT])
        bp_bc = sb("bp_bc", [T, E])
        g2_bc = sb("g2_bc", [T, E])
        b2_bc = sb("b2_bc", [T, E])
        wqk = sb("wqk", [EH, 2, 8, HPAD])
        wo = sb("wo", [EH, 2, E])
        w1 = sb("w1", [EH + 1, 2, F])
        w2 = sb("w2", [128, M, E])
        a1 = sb("a1", [EH + 1, NE, 2, F])
        a2 = sb("a2", [128, NE, M, E])
        a2b = sb("a2b", [1, NE, E])
        gw = sb("gw", [EH, 2, NCLS, 2])
        ident = sb("ident", [128, 128])
        ones = sb("ones", [T, 128])
        neg_half = sb("neg_half", [T, G])
        img_mask = sb("img_mask", [T, B])
        row_mask = sb("row_mask", [T, G])
        cls_mask = sb("cls_mask", [T, NCLS])
        slot_mask = sb("slot_mask", [QR, SLOTS])
        x_buf = sb("x_buf", [128, C * PATCH * IMG])
        x_sb = x_buf[0:B * G, :].rearrange("p (c f) -> p c f", c=C)
        xr_buf = sb("xr_buf", [128, C * G * PATCH * PATCH])
        x_r = xr_buf[0:B * G, :].rearrange("p (c w f) -> p c w f", c=C, w=G)
        xT_buf = sb("xT_buf", [128, KT * NTOK])
        xT = xT_buf[:].rearrange("p (k n) -> p k n", k=KT)
        squares = sb("squares", [B * G, C, PATCH, PATCH])
        ss = sb("ss", [B * G, G])
        ss_diag = sb("ss_diag", [B * G, G, B])
        ms1 = sb("ms1", [T, G])
        r1 = sb("r1", [T, G])
        y = sb("y", [T, G, E])
        y_sq = sb("y_sq", [T, E])
        ms2 = sb("ms2", [T, G])
        ms2e = sb("ms2e", [T, G])
        r2 = sb("r2", [T, G])
        h0 = sb("h0", [T, G, E])
        stats = sb("stats", [T, 2, G, 6])
        mv = sb("mv", [T, 2, G, 2])
        ve = sb("ve", [T, 2, G])
        rs = sb("rs", [T, 2, G])
        xn = sb("xn", [T, G, E])
        xnT = sb("xnT", [EH, 2, B, N])
        q_bd = xr_buf[0:QR, 0:2 * B * SP].rearrange("r (p b s n) -> r p b s n", p=2, b=B, s=SLOTS)
        k_bd = sb("k_bd", [QR, 2, B, 2, HPAD])
        s_max = sb("s_max", [SP, 2, 8])
        s_sub = sb("s_sub", [SP, 2, 8, N])
        e_sb = sb("e_sb", [SP, 2, 8, N])
        e_sum = sb("e_sum", [SP, 2, 8])
        e_inv = sb("e_inv", [SP, 2, 8])
        p_sb = sb("p_sb", [SP, 2, 8, HPAD])
        pT = sb("pT", [PR, 2, 4, SP])
        kp = sb("kp", [PR, 2, 4, SLOTS, 2, D])
        oT = sb("oT", [EH, 2, N, B])
        h1 = sb("h1", [T, G, E])
        h1b = y
        xn2 = sb("xn2", [T, G, E])
        x2T = sb("x2T", [EH + 1, 2, NTOK])
        hT = x_buf[:, 0:M * (NTOK - T)].rearrange("p (m n) -> p m n", m=M)
        heT = xT_buf[:, 0:M * HT].rearrange("p (m n) -> p m n", m=M)
        heG = xT_buf[:, M * HT:2 * M * HT].rearrange("p (m n) -> p m n", m=M)
        lg6 = sb("lg6", [T, 2, NCLS])
        lg = sb("lg", [T, 2])
        gs = sb("gs", [T, 8])
        ge = sb("ge", [T, 2])
        gp = sb("gp", [T, 2])
        gk = sb("gk", [T, 2])
        gm = sb("gm", [T, 2])
        gn = sb("gn", [T, 2])
        g_diag = sb("g_diag", [T, HT])
        gb = sb("gb", [128, HT])
        clsT = sb("clsT", [EH, 2, T])
        res = xn

        x_in = [sem(f"x_in{c}") for c in range(C)]
        wp_in, vec_in, wqk_in, wo_in, w1_in, a1_in, gw_in, w2_in, a2_in = (
            sem(n) for n in ("wp_in", "vec_in", "wqk_in", "wo_in", "w1_in", "a1_in", "gw_in", "w2_in", "a2_in"))
        out_done = sem("out_done")
        consts, wpg_ready, r1_ready, r2_ready, rs_ready, p_ready, h1b_ready, pool_step = (
            sem(n) for n in ("consts", "wpg_ready", "r1_ready", "r2_ready", "rs_ready", "p_ready", "h1b_ready",
                             "pool_step"))
        xt_ps, r1_ps, emb_ps, ln1_ps, qk_ps, s_ps, kp_ps, pt_ps, pv_ps, wo_ps, ln2_ps, gate_ps, a1_ps, gb_ps, f1_ps, \
            a2_ps, f2_ps, cls_ps = (
                sem(n) for n in ("xt_ps", "r1_ps", "emb_ps", "ln1_ps", "qk_ps", "s_ps", "kp_ps", "pt_ps", "pv_ps",
                                 "wo_ps", "ln2_ps", "gate_ps", "a1_ps", "gb_ps", "f1_ps", "a2_ps", "f2_ps", "cls_ps"))
        masks, xr_ready, xt_ready, diag_ready, ms1_ready, y_ready, h0_ready, stat_ready, mv_ready, xn_ready, q_ready, max_ready, \
            sub_ready, sum_ready, inv_ready, ov_ready, h1_ready, xn2_ready, gate_step, gd_ready, heg_ready, \
            clsT_ready, res_ready = (
                sem(n) for n in ("masks", "xr_ready", "xt_ready", "diag_ready", "ms1_ready", "y_ready", "h0_ready", "stat_ready",
                                 "mv_ready", "xn_ready", "q_ready", "max_ready", "sub_ready", "sum_ready",
                                 "inv_ready", "ov_ready", "h1_ready", "xn2_ready", "gate_step", "gd_ready",
                                 "heg_ready", "clsT_ready", "res_ready"))
        ss_ready, ms2_ready, xnT_ready, k_ready, e_ready, pT_ready, kp_ready, oa_ready, x2T_ready, ge_ready, \
            he_ready, gb_ready, h_ready = (
                sem(n) for n in ("ss_ready", "ms2_ready", "xnT_ready", "k_ready", "e_ready", "pT_ready", "kp_ready",
                                 "oa_ready", "x2T_ready", "ge_ready", "he_ready", "gb_ready", "h_ready"))

        block = ctx.enter_context(nc.Block())

        @block.sync
        def _(sp):
            x_rows = x.rearrange("b c (h p) w -> c b h (p w)", p=PATCH)
            w_rows = wp.rearrange("(q p c) e -> p q (c e)", q=2, c=C)
            sp.dma_start(x_sb[:, 0, :], x_rows[0]).then_inc(x_in[0], 16)
            sp.dma_start(wp_g[:].rearrange("p (q c) e -> p q (c e)", q=2), w_rows).then_inc(wp_in, 16)
            sp.dma_start(g1_sb[:].rearrange("p (q c) -> p q c", q=2),
                         g1.rearrange("(q p c) -> p q c", q=2, c=C)).then_inc(wp_in, 16)
            for c in range(1, C):
                sp.dma_start(x_sb[:, c, :], x_rows[c]).then_inc(x_in[c], 16)
            for vec, dst in ((bp, bp_bc), (g2, g2_bc), (moe_b2, b2_bc)):
                sp.dma_start(dst[:], vec.rearrange("(o e) -> o e", o=1).broadcast_to([T, E])).then_inc(vec_in, 16)
            for k in range(2):
                sp.dma_start(wqk[:, k, :, 0:HALF], w_qkv[k * EH:(k + 1) * EH, 0:2 * E]
                             .rearrange("r (g f) -> r g f", f=HALF)).then_inc(wqk_in, 16)
            wo_rows = w_out.rearrange("(p g s d) e -> s p g d e", p=2, g=2, s=SLOTS)
            for s in range(SLOTS):
                for p in range(2):
                    sp.dma_start(wo[2 * D * s:2 * D * (s + 1), p, :], wo_rows[s, p]).then_inc(wo_in, 16)
            for k in range(2):
                sp.dma_start(gw[:, k, :, :], g_w[:, k * EH:(k + 1) * EH, :].rearrange("i r g -> r i g")) \
                    .then_inc(gw_in, 16)
            a1_rows = a1_w.rearrange("a (k r) f -> a r k f", k=2)
            for a in range(NE):
                sp.dma_start(a1[0:EH, a, :, :], a1_rows[a]).then_inc(a1_in, 16)
            sp.dma_start(a1[EH:EH + 1, :, 0, :], a1_b.rearrange("(o a) f -> o a f", o=1)).then_inc(a1_in, 16)
            sp.dma_start(w1[0:EH, :, :], moe_w1.rearrange("(k r) f -> r k f", k=2)).then_inc(w1_in, 16)
            sp.dma_start(w1[EH:EH + 1, 0, :], moe_b1.rearrange("(o f) -> o f", o=1)).then_inc(w1_in, 16)
            sp.dma_start(a2b[:], a2_b.rearrange("(o a) e -> o a e", o=1)).then_inc(a2_in, 16)
            a2_rows = a2_w.rearrange("a (m r) e -> a r m e", m=M)
            for a in range(NE):
                sp.dma_start(a2[:, a, :, :], a2_rows[a]).then_inc(a2_in, 16)
            sp.dma_start(w2[:], moe_w2.rearrange("(m r) e -> r m e", m=M)).then_inc(w2_in, 16)
            out_rows = out.rearrange("b (t w) e -> t w b e", t=G)
            for n, t in enumerate((1, 0, 2, 3, 4, 5)):
                sp.wait_ge(res_ready, n + 1)
                sp.dma_start(out_rows[t], res[:, t, :]).then_inc(out_done, 16)
            sp.wait_ge(out_done, 16 * G)

        @block.gpsimd
        def _(pool):
            nc.gpsimd.memset(ident[:], 0.0).then_inc(pool_step, 1)
            pool.wait_ge(pool_step, 1)
            nc.gpsimd.affine_select(out=ident[:], in_=ident[:], compare_op=ALU.not_equal, fill=1.0, base=0,
                                    pattern=[[-1, 128]], channel_multiplier=1).then_inc(consts, 1)
            pool.wait_ge(wp_in, 32)
            nc.gpsimd.tensor_tensor(wp_g[:], wp_g[:], g1_sb[:].rearrange("p (k o) -> p k o", o=1)
                                    .broadcast_to([128, KT, E]), ALU.mult).then_inc(wpg_ready, 1)
            nc.gpsimd.memset(neg_half[:], -0.5).then_inc(consts, 1)
            nc.gpsimd.memset(ones[:], 1.0).then_inc(consts, 1)
            nc.gpsimd.memset(wqk[:, :, :, HALF:HPAD], 0.0).then_inc(consts, 1)
            nc.gpsimd.memset(p_sb[:], 0.0).then_inc(consts, 1)
            nc.gpsimd.memset(k_bd[:], 0.0).then_inc(consts, 1)
            pool.wait_ge(consts, 6)
            pool.wait_ge(ms1_ready, 1)
            nc.gpsimd.tensor_tensor(r1[:], ms1[:], neg_half[:], ALU.pow).then_inc(r1_ready, 1)
            step = 1

            def inv_sqrt(dst, src, tmp, scale, eps, done):
                nonlocal step
                nc.gpsimd.tensor_scalar(tmp, src, scale, eps, ALU.mult, ALU.add).then_inc(pool_step, 1)
                step += 1
                pool.wait_ge(pool_step, step)
                nc.gpsimd.tensor_tensor(dst, tmp, neg_half[:, 0:2], ALU.pow).then_inc(done, 1)

            def rms2(g):
                pool.wait_ge(ms2_ready, 2 * g + 2)
                inv_sqrt(r2[:, 2 * g:2 * g + 2], ms2[:, 2 * g:2 * g + 2], ms2e[:, 2 * g:2 * g + 2], 1.0 / E, EPS_RMS,
                         r2_ready)

            def norm(w, g):
                pool.wait_ge(mv_ready, 2 * (PAIRS * w + g) + 2)
                inv_sqrt(rs[:, w, 2 * g:2 * g + 2], mv[:, w, 2 * g:2 * g + 2, 1], ve[:, w, 2 * g:2 * g + 2], 1.0,
                         EPS_LN, rs_ready)

            rms2(0)
            norm(0, 0)
            rms2(1)
            norm(0, 1)
            rms2(2)
            norm(0, 2)
            for u in range(NU):
                pool.wait_ge(inv_ready, u + 1)
                if u >= 2:
                    pool.wait_ge(pt_ps, u - 1)
                nc.gpsimd.tensor_tensor(p_sb[:, u % 2, :, 0:N], e_sb[:, u % 2, :, :],
                                        e_inv[:, u % 2, :].rearrange("p (k o) -> p k o", o=1)
                                        .broadcast_to([SP, 8, N]), ALU.mult).then_inc(p_ready, 1)
            for g in range(PAIRS):
                norm(1, g)
            pool.wait_ge(vec_in, 48)
            pool.wait_ge(h1_ready, G)
            nc.gpsimd.tensor_tensor(h1b[:, 1:G, :], h1[:, 1:G, :], b2_bc[:].rearrange("p (o e) -> p o e", o=1)
                                    .broadcast_to([T, G - 1, E]), ALU.add).then_inc(h1b_ready, 1)

        @block.tensor
        def _(pe):
            pe.wait_ge(consts, 1)

            def transpose_patches(kt):
                c, q = kt // 2, kt % 2
                if q == 0:
                    pe.wait_ge(xr_ready, c + 1)
                for half in range(2):
                    f = 2 * kt + half
                    if f >= 2:
                        pe.wait_ge(xt_ready, f - 1)
                    for w in range(3):
                        last = nc.tensor.transpose(bank[XT_BANK[f % 2]][:, w * T:(w + 1) * T], x_r[:, c, 3 * half + w, q * 128:(q + 1) * 128],
                                                   ident[0:T, 0:T])
                    last.then_inc(xt_ps, 1)

            def embed(kt, t):
                return nc.tensor.matmul(bank[EMB_BANK[t]][0:T, 0:E], xT[:, kt, t * T:(t + 1) * T],
                                        wp_g[:, (kt % 2) * C + kt // 2, :], start=(kt == 0), stop=(kt == KT - 1))

            transpose_patches(0)
            pe.wait_ge(wpg_ready, 1)
            for kt in range(KT):
                if kt + 1 < KT:
                    transpose_patches(kt + 1)
                if kt < KT - 2:
                    pe.wait_ge(xt_ready, 2 * kt + 2)
                    for t in range(G):
                        embed(kt, t)
            pe.wait_ge(xt_ready, 2 * KT)
            pe.wait_ge(diag_ready, 1)
            nc.tensor.matmul(bank[R1_BANK][0:T, 0:G], ss_diag[:].rearrange("p w b -> p (w b)"), row_mask[:],
                             start=True, stop=True).then_inc(r1_ps, 1)
            for t in range(G):
                embed(KT - 2, t)
                embed(KT - 1, t).then_inc(emb_ps, 1)

            for t in range(G):
                pe.wait_ge(xn_ready, t + 1)
                if t == 0:
                    pe.wait_ge(ms1_ready, 1)
                if t >= 2:
                    pe.wait_ge(xnT_ready, t - 1)
                for k in range(2):
                    last = nc.tensor.transpose(bank[LN1_BANK[t % 2]][0:EH, k * T:(k + 1) * T],
                                               xn[:, t, k * EH:(k + 1) * EH], ident[0:T, 0:T])
                last.then_inc(ln1_ps, 1)

            pe.wait_ge(xnT_ready, G)
            pe.wait_ge(wqk_in, 32)
            pe.wait_ge(consts, 6)
            o = 0
            for ch in range(B // CHUNK):
                for s in range(4):
                    if o >= len(QK_BANK):
                        pe.wait_ge(q_ready, o - len(QK_BANK) + 1)
                    for k in range(2):
                        last = nc.tensor.matmul(
                            bank[QK_BANK[o % len(QK_BANK)]][0:QR, 0:CHUNK * N],
                            wqk[:, k, 2 * s:2 * s + 2, :].rearrange("r g f -> r (g f)")[:, 0:QR],
                            xnT[:, k, ch * CHUNK:(ch + 1) * CHUNK, :].rearrange("r b n -> r (b n)"),
                            start=(k == 0), stop=(k == 1))
                    last.then_inc(qk_ps, 1)
                    o += 1

            def scores(u):
                ch = u * UNIT // CHUNK
                pe.wait_ge(q_ready, 2 * (ch + 1))
                pe.wait_ge(k_ready, 4 * (ch + 1))
                if u >= 2:
                    pe.wait_ge(sub_ready, u - 1)
                for i in range(UNIT):
                    for p in range(2):
                        n = 2 * i + p
                        last = nc.tensor.matmul(bank[S_BANK[u % 2]][0:SP, n * SC:(n + 1) * SC],
                                                q_bd[:, p, u * UNIT + i, :, :].rearrange("r s n -> r (s n)"),
                                                k_bd[:, p, u * UNIT + i, :, 0:N], start=True, stop=True)
                last.then_inc(s_ps, 1)

            def keys(u):
                pe.wait_ge(k_ready, 4 * (u * UNIT // CHUNK + 1))
                if u >= 2:
                    pe.wait_ge(kp_ready, 2 * (u - 1))
                for i in range(UNIT):
                    for p in range(2):
                        n = 2 * i + p
                        last = nc.tensor.transpose(
                            bank[KP_BANK[u % 2]][0:PR, n * QR:(n + 1) * QR],
                            k_bd[:, p, u * UNIT + i, :, :].rearrange("r g j -> r (g j)")[:, 0:PR], ident[0:QR, 0:QR])
                last.then_inc(kp_ps, 1)

            def probs(u):
                pe.wait_ge(p_ready, u + 1)
                if u == 0:
                    pe.wait_ge(q_ready, 4)
                if u >= 2:
                    pe.wait_ge(pT_ready, u - 1)
                for n in range(2 * UNIT):
                    last = nc.tensor.transpose(
                        bank[PT_BANK[u % 2]][0:PR, n * SP:(n + 1) * SP],
                        p_sb[:, u % 2, 2 * n:2 * n + 2, :].rearrange("r g j -> r (g j)")[:, 0:PR], ident[0:SP, 0:SP])
                last.then_inc(pt_ps, 1)

            def values(u):
                pe.wait_ge(pT_ready, u + 1)
                pe.wait_ge(kp_ready, 2 * (u + 1))
                if u == 0:
                    pe.wait_ge(k_ready, 8)
                if u >= 2:
                    pe.wait_ge(ov_ready, 2 * (u - 1))
                    pe.wait_ge(oa_ready, u - 1)
                for n in range(2 * UNIT):
                    last = nc.tensor.matmul(bank[PV_BANK[u % 2]][0:EH, n * SP:(n + 1) * SP],
                                            kp[:, u % 2, n].rearrange("r s g d -> r (s g d)"),
                                            pT[:, u % 2, n, :], start=True, stop=True)
                last.then_inc(pv_ps, 1)

            scores(0)
            scores(1)
            keys(0)
            for u in range(NU):
                probs(u)
                if u + 2 < NU:
                    scores(u + 2)
                if u + 1 < NU:
                    keys(u + 1)
                values(u)

            pe.wait_ge(ov_ready, 2 * NU)
            pe.wait_ge(oa_ready, NU)
            pe.wait_ge(wo_in, 96)
            for t in range(G):
                if t >= len(WO_BANK):
                    pe.wait_ge(h1_ready, t - len(WO_BANK) + 1)
                for p in range(2):
                    last = nc.tensor.matmul(bank[WO_BANK[t % len(WO_BANK)]][0:T, 0:E],
                                            oT[:, p, t * G:(t + 1) * G, :].rearrange("r n b -> r (n b)"),
                                            wo[:, p, :], start=(p == 0), stop=(p == 1))
                last.then_inc(wo_ps, 1)

            def transpose_ln2(t):
                pe.wait_ge(xn2_ready, t + 1)
                if t >= 2:
                    pe.wait_ge(x2T_ready, t - 1)
                for k in range(2):
                    last = nc.tensor.transpose(bank[LN2_BANK[t % 2]][0:EH, k * T:(k + 1) * T],
                                               xn2[:, t, k * EH:(k + 1) * EH], ident[0:T, 0:T])
                last.then_inc(ln2_ps, 1)

            def expert_hidden(a):
                pe.wait_ge(a1_in, 16 * (NE + 1))
                if a == 1:
                    pe.wait_ge(gate_step, 1)
                if a >= 2:
                    pe.wait_ge(he_ready, a - 1)
                n = EXPERT_TOK[a]
                for m in range(M):
                    for k in range(2):
                        rows = EH + 1 - k
                        if a < 3:
                            tok = x2T[0:rows, k, a * n:(a + 1) * n]
                        else:
                            tok = x2T[0:rows, k, 0:T].rearrange("r (u v b) -> r u v b", u=3, v=2)[:, :, a - 3, :]
                        last = nc.tensor.matmul(bank[A1_BANK[a % 2]][:, m * n:(m + 1) * n],
                                                a1[0:rows, a, k, m * 128:(m + 1) * 128], tok,
                                                start=(k == 0), stop=(k == 1))
                last.then_inc(a1_ps, 1)

            transpose_ln2(0)
            pe.wait_ge(x2T_ready, 1)
            pe.wait_ge(gw_in, 32)
            pe.wait_ge(masks, 5)
            for k in range(2):
                last = nc.tensor.matmul(bank[GATE_BANK][0:T, 0:2 * NCLS], x2T[0:EH, k, 0:T],
                                        gw[:, k, :, :].rearrange("r i g -> r (i g)"), start=(k == 0), stop=(k == 1))
            last.then_inc(gate_ps, 1)
            for a in range(NE):
                expert_hidden(a)
                transpose_ln2(a + 1)
            pe.wait_ge(gd_ready, 2)
            nc.tensor.matmul(bank[GB_BANK][:, 0:HT], ones[:], g_diag[:], start=True, stop=True).then_inc(gb_ps, 1)
            pe.wait_ge(x2T_ready, G)
            pe.wait_ge(w1_in, 32)
            for m in range(M):
                if m >= 2:
                    pe.wait_ge(h_ready, m - 1)
                for k in range(2):
                    rows = EH + 1 - k
                    last = nc.tensor.matmul(bank[F1_BANK[m % 2]][:, 0:NTOK - T], w1[0:rows, k, m * 128:(m + 1) * 128],
                                            x2T[0:rows, k, T:NTOK], start=(k == 0), stop=(k == 1))
                last.then_inc(f1_ps, 1)
            pe.wait_ge(heg_ready, 1)
            pe.wait_ge(a2_in, 16 * (NE + 1))
            first = True
            for k in range(2):
                for c in (3, 4, 0, 1, 2):
                    for m in range(M + 1):
                        src = heG[:, m, :] if m < M else gb[0:1, :]
                        if c >= 3:
                            tok = src[:, 0:T].rearrange("r (u v b) -> r u v b", u=3, v=2)[:, :, c - 3, :]
                            dst = bank[A2_BANK][0:EH, k * T:(k + 1) * T] \
                                .rearrange("r (u v b) -> r u v b", u=3, v=2)[:, :, c - 3, :]
                        else:
                            tok = src[:, T:HT].rearrange("r (v u b) -> r v u b", v=2, u=3)[:, :, c, :]
                            dst = bank[A2_BANK][0:EH, k * T + 32 * c:k * T + 32 * (c + 1)]
                        wgt = a2[:, c, m, k * EH:(k + 1) * EH] if m < M else a2b[:, c, k * EH:(k + 1) * EH]
                        last = nc.tensor.matmul(dst, wgt, tok, start=first, stop=(m == M), skip_group_check=True)
                        first = False
            last.then_inc(a2_ps, 1)
            pe.wait_ge(h_ready, M)
            pe.wait_ge(w2_in, 16)
            for t in range(1, G):
                if t >= 3:
                    pe.wait_ge(res_ready, t - 1 if t == 3 else t - 1)
                for m in range(M):
                    last = nc.tensor.matmul(bank[F2_BANK[t % 2]][0:T, 0:E], hT[:, m, (t - 1) * T:t * T], w2[:, m, :],
                                            start=(m == 0), stop=(m == M - 1))
                last.then_inc(f2_ps, 1)
                if t == 1:
                    pe.wait_ge(clsT_ready, 1)
                    for k in range(2):
                        last = nc.tensor.transpose(bank[CLS_BANK][0:T, k * EH:(k + 1) * EH], clsT[:, k, :],
                                                   ident[0:EH, 0:EH])
                    last.then_inc(cls_ps, 1)

        @block.scalar
        def _(act):
            for c in range(C):
                act.wait_ge(x_in[c], 16)
            patches = x_sb.rearrange("p c (r w f) -> p w c r f", r=PATCH, w=G)
            for w in range(G):
                if w >= 1:
                    act.wait_ge(ss_ready, w)
                nc.scalar.activation(squares[:], patches[:, w], ACT.Square,
                                     accum_out=ss[:, w:w + 1]).then_inc(ss_ready, 1)
            for t in range(G):
                act.wait_ge(y_ready, t + 1)
                if t >= 1:
                    act.wait_ge(ms2_ready, t)
                nc.scalar.activation(y_sq[:], y[:, t, :], ACT.Square, accum_out=ms2[:, t:t + 1]).then_inc(ms2_ready, 1)
            for t in range(G):
                act.wait_ge(ln1_ps, t + 1)
                nc.scalar.activation(xnT[:, :, :, t * G:(t + 1) * G].rearrange("r k b n -> r k n b"),
                                     bank[LN1_BANK[t % 2]][0:EH, 0:2 * T].rearrange("r (k n b) -> r k n b", k=2, n=G),
                                     ACT.Copy).then_inc(xnT_ready, 1)
            act.wait_ge(consts, 6)
            for ch in range(B // CHUNK):
                for p in range(2):
                    o = 4 * ch + 2 + p
                    act.wait_ge(qk_ps, o + 1)
                    src = bank[QK_BANK[o % len(QK_BANK)]]
                    for hg in range(2):
                        rows = slice(hg * HPAD, hg * HPAD + HALF)
                        nc.scalar.activation(k_bd[rows, p, ch * CHUNK:(ch + 1) * CHUNK, hg, 0:N],
                                             src[rows, 0:CHUNK * N].rearrange("r (b n) -> r b n", b=CHUNK),
                                             ACT.Copy).then_inc(k_ready, 1)

            def exponentials(u):
                act.wait_ge(sub_ready, u + 1)
                if u >= 2:
                    act.wait_ge(p_ready, u - 1)
                    act.wait_ge(sum_ready, u - 1)
                nc.scalar.activation(e_sb[:, u % 2, :, :], s_sub[:, u % 2, :, :], ACT.Exp,
                                     scale=float(E) ** -0.5).then_inc(e_ready, 1)

            def copy_keys(u):
                act.wait_ge(kp_ps, u + 1)
                if u >= 2:
                    act.wait_ge(pv_ps, u - 1)
                src = bank[KP_BANK[u % 2]][0:PR, 0:4 * QR].rearrange("r (n c) -> r n c", n=4)
                for hg in range(2):
                    nc.scalar.activation(kp[:, u % 2, :, :, hg, :], src[:, :, hg * HPAD:hg * HPAD + HALF]
                                         .rearrange("r n (s d) -> r n s d", s=SLOTS), ACT.Copy).then_inc(kp_ready, 1)

            def copy_probs(u):
                act.wait_ge(pt_ps, u + 1)
                if u >= 2:
                    act.wait_ge(pv_ps, u - 1)
                nc.scalar.activation(pT[:, u % 2, :, :], bank[PT_BANK[u % 2]][0:PR, 0:4 * SP]
                                     .rearrange("r (n c) -> r n c", n=4), ACT.Copy).then_inc(pT_ready, 1)

            def take_values(u):
                act.wait_ge(pv_ps, u + 1)
                nc.scalar.activation(*value_block(oT, bank, u, 0), ACT.Copy).then_inc(oa_ready, 1)

            exponentials(0)
            copy_keys(0)
            for u in range(NU):
                if u + 1 < NU:
                    exponentials(u + 1)
                copy_probs(u)
                if u + 1 < NU:
                    copy_keys(u + 1)
                take_values(u)

            def copy_ln2(t):
                act.wait_ge(ln2_ps, t + 1)
                nc.scalar.activation(x2T[0:EH, :, t * T:(t + 1) * T],
                                     bank[LN2_BANK[t % 2]][0:EH, 0:2 * T].rearrange("r (k c) -> r k c", k=2),
                                     ACT.Copy).then_inc(x2T_ready, 1)

            copy_ln2(0)
            act.wait_ge(gate_step, 4)
            nc.scalar.activation(ge[:], gs[:, 1:3], ACT.Exp).then_inc(ge_ready, 1)
            for a in range(NE):
                act.wait_ge(a1_ps, a + 1)
                n = EXPERT_TOK[a]
                nc.scalar.activation(heT[:, :, EXPERT_COLS[a]:EXPERT_COLS[a] + n],
                                     bank[A1_BANK[a % 2]][:, 0:M * n].rearrange("r (m c) -> r m c", m=M),
                                     ACT.Gelu).then_inc(he_ready, 1)
                copy_ln2(a + 1)
            act.wait_ge(gb_ps, 1)
            nc.scalar.activation(gb[:], bank[GB_BANK][:, 0:HT], ACT.Copy).then_inc(gb_ready, 1)
            for m in range(M):
                act.wait_ge(f1_ps, m + 1)
                nc.scalar.activation(hT[:, m, :], bank[F1_BANK[m % 2]][:, 0:NTOK - T], ACT.Gelu).then_inc(h_ready, 1)

        @block.vector
        def _(dve):
            dve.wait_ge(consts, 1)
            nc.vector.tensor_reduce(img_mask[:], ident[0:T, 0:T].rearrange("p (b h) -> p b h", b=B), AX.X,
                                    ALU.add).then_inc(masks, 1)
            nc.vector.tensor_reduce(row_mask[:], ident[0:T, 0:T].rearrange("p (b h) -> p h b", b=B), AX.X,
                                    ALU.add).then_inc(masks, 1)
            nc.vector.tensor_reduce(cls_mask[:], ident[0:T, 0:T].rearrange("p (i b) -> p i b", i=NCLS), AX.X,
                                    ALU.add).then_inc(masks, 1)
            nc.vector.tensor_reduce(
                slot_mask[:], ident[0:QR, :].rearrange("p (g f) -> p g f", g=2)[:, :, 0:HALF]
                .rearrange("p g (s d) -> p s g d", s=SLOTS), AX.XY, ALU.add).then_inc(masks, 1)
            nc.vector.memset(x2T[EH:EH + 1, 0, :], 1.0).then_inc(masks, 1)

            def regroup(c):
                dve.wait_ge(x_in[c], 16)
                nc.vector.tensor_copy(x_r[:, c, :, :].rearrange("p w (r f) -> p w r f", r=PATCH),
                                      x_sb[:, c, :].rearrange("p (r w f) -> p w r f", r=PATCH, w=G)) \
                    .then_inc(xr_ready, 1)

            regroup(0)
            for f in range(2 * KT):
                if f in (2, 6):
                    regroup(f // 4 + 1)
                kt, half = f // 2, f % 2
                dve.wait_ge(xt_ps, f + 1)
                nc.vector.tensor_copy(
                    xT[:, kt, :].rearrange("r (h w b) -> r w b h", h=G, w=G)[:, 3 * half:3 * half + 3],
                    bank[XT_BANK[f % 2]][:, 0:3 * T].rearrange("r (w b h) -> r w b h", w=3, b=B)).then_inc(xt_ready, 1)

            dve.wait_ge(ss_ready, G)
            dve.wait_ge(masks, 4)
            nc.vector.tensor_tensor(ss_diag[:], ss[:].rearrange("p (w o) -> p w o", o=1).broadcast_to([T, G, B]),
                                    img_mask[:].rearrange("p (o b) -> p o b", o=1).broadcast_to([T, G, B]),
                                    ALU.mult).then_inc(diag_ready, 1)
            dve.wait_ge(r1_ps, 1)
            nc.vector.tensor_scalar(ms1[:], bank[R1_BANK][0:T, 0:G], 1.0 / PD, EPS_RMS, ALU.mult,
                                    ALU.add).then_inc(ms1_ready, 1)
            dve.wait_ge(vec_in, 48)

            def embedded(g):
                for t in (2 * g, 2 * g + 1):
                    dve.wait_ge(emb_ps, t + 1)
                    if t == 0:
                        dve.wait_ge(r1_ready, 1)
                    nc.vector.scalar_tensor_tensor(out=y[:, t, :], in0=bank[EMB_BANK[t]][0:T, 0:E],
                                                   scalar=r1[:, t:t + 1], in1=bp_bc[:], op0=ALU.mult,
                                                   op1=ALU.add).then_inc(y_ready, 1)

            def statistics(w, h, t, ready):
                dve.wait_ge(ready, t + 1)
                nc.vector.bn_stats(stats[:, w, t, :], h[:, t, :]).then_inc(stat_ready, 1)

            def moments(w, t):
                dve.wait_ge(stat_ready, G * w + t + 1)
                nc.vector.bn_aggr(mv[:, w, t, :], stats[:, w, t, :]).then_inc(mv_ready, 1)

            def normalise(w, h, dst, g, ready):
                dve.wait_ge(rs_ready, PAIRS * w + g + 1)
                for t in (2 * g, 2 * g + 1):
                    nc.vector.tensor_scalar(dst[:, t, :], h[:, t, :], mv[:, w, t, 0:1], rs[:, w, t:t + 1],
                                            ALU.subtract, ALU.mult).then_inc(ready, 1)

            def hidden0(g):
                dve.wait_ge(r2_ready, g + 1)
                for t in (2 * g, 2 * g + 1):
                    nc.vector.scalar_tensor_tensor(out=h0[:, t, :], in0=y[:, t, :], scalar=r2[:, t:t + 1],
                                                   in1=g2_bc[:], op0=ALU.mult, op1=ALU.mult).then_inc(h0_ready, 1)
                for t in (2 * g, 2 * g + 1):
                    statistics(0, h0, t, h0_ready)
                for t in (2 * g, 2 * g + 1):
                    moments(0, t)

            embedded(0)
            dve.wait_ge(y_ready, 2)
            embedded(1)
            hidden0(0)
            embedded(2)
            normalise(0, h0, xn, 0, xn_ready)
            dve.wait_ge(y_ready, 6)
            hidden0(1)
            normalise(0, h0, xn, 1, xn_ready)
            hidden0(2)
            normalise(0, h0, xn, 2, xn_ready)

            for ch in range(B // CHUNK):
                for p in range(2):
                    o = 4 * ch + p
                    dve.wait_ge(qk_ps, o + 1)
                    nc.vector.tensor_tensor(
                        q_bd[:, p, ch * CHUNK:(ch + 1) * CHUNK, :, :],
                        bank[QK_BANK[o % len(QK_BANK)]][0:QR, 0:CHUNK * N].rearrange("r (b o n) -> r b o n", b=CHUNK, o=1)
                        .broadcast_to([QR, CHUNK, SLOTS, N]),
                        slot_mask[:].rearrange("r (o s q) -> r o s q", o=1, q=1)
                        .broadcast_to([QR, CHUNK, SLOTS, N]), ALU.mult).then_inc(q_ready, 1)

            def row_max(u):
                dve.wait_ge(s_ps, u + 1)
                s = bank[S_BANK[u % 2]][0:SP, 0:8 * N].rearrange("p (k j) -> p k j", k=8)
                if u >= 2:
                    dve.wait_ge(sub_ready, u - 1)
                nc.vector.tensor_reduce(s_max[:, u % 2, :], s, AX.X, ALU.max).then_inc(max_ready, 1)

            def subtract_max(u):
                dve.wait_ge(max_ready, u + 1)
                if u >= 2:
                    dve.wait_ge(e_ready, u - 1)
                s = bank[S_BANK[u % 2]][0:SP, 0:8 * N].rearrange("p (k j) -> p k j", k=8)
                nc.vector.tensor_tensor(s_sub[:, u % 2, :, :], s, s_max[:, u % 2, :]
                                        .rearrange("p (k o) -> p k o", o=1).broadcast_to([SP, 8, N]),
                                        ALU.subtract).then_inc(sub_ready, 1)

            def row_sum(u):
                dve.wait_ge(e_ready, u + 1)
                if u >= 2:
                    dve.wait_ge(inv_ready, u - 1)
                nc.vector.tensor_reduce(e_sum[:, u % 2, :], e_sb[:, u % 2, :, :], AX.X, ALU.add).then_inc(sum_ready, 1)

            def invert_sum(u):
                dve.wait_ge(sum_ready, u + 1)
                if u >= 2:
                    dve.wait_ge(p_ready, u - 1)
                nc.vector.reciprocal(e_inv[:, u % 2, :], e_sum[:, u % 2, :]).then_inc(inv_ready, 1)

            def take_values(u):
                dve.wait_ge(pv_ps, u + 1)
                for s in (1, 2):
                    dst, src = value_block(oT, bank, u, s)
                    nc.vector.tensor_copy(dst, src).then_inc(ov_ready, 1)

            row_max(0)
            subtract_max(0)
            for u in range(NU):
                if u + 1 < NU:
                    row_max(u + 1)
                row_sum(u)
                if u + 1 < NU:
                    subtract_max(u + 1)
                invert_sum(u)
                if u >= 1:
                    take_values(u - 1)
            take_values(NU - 1)

            def residual(g):
                for t in (2 * g, 2 * g + 1):
                    dve.wait_ge(wo_ps, t + 1)
                    nc.vector.tensor_tensor(h1[:, t, :], bank[WO_BANK[t % len(WO_BANK)]][0:T, 0:E], h0[:, t, :],
                                            ALU.add).then_inc(h1_ready, 1)
                for t in (2 * g, 2 * g + 1):
                    statistics(1, h1, t, h1_ready)
                for t in (2 * g, 2 * g + 1):
                    moments(1, t)

            residual(0)
            residual(1)
            normalise(1, h1, xn2, 0, xn2_ready)
            residual(2)
            normalise(1, h1, xn2, 1, xn2_ready)
            normalise(1, h1, xn2, 2, xn2_ready)

            dve.wait_ge(gate_ps, 1)
            nc.vector.tensor_tensor(lg6[:], bank[GATE_BANK][0:T, 0:2 * NCLS].rearrange("p (i g) -> p g i", g=2),
                                    cls_mask[:].rearrange("p (o i) -> p o i", o=1).broadcast_to([T, 2, NCLS]),
                                    ALU.mult).then_inc(gate_step, 1)
            dve.wait_ge(gate_step, 1)
            nc.vector.tensor_reduce(lg[:], lg6[:], AX.X, ALU.add).then_inc(gate_step, 1)
            dve.wait_ge(gate_step, 2)
            nc.vector.tensor_reduce(gs[:, 0:1], lg[:], AX.X, ALU.max).then_inc(gate_step, 1)
            dve.wait_ge(gate_step, 3)
            nc.vector.tensor_scalar(gs[:, 1:3], lg[:], gs[:, 0:1], None, ALU.subtract).then_inc(gate_step, 1)
            dve.wait_ge(ge_ready, 1)
            nc.vector.tensor_reduce(gs[:, 3:4], ge[:], AX.X, ALU.add).then_inc(gate_step, 1)
            dve.wait_ge(gate_step, 5)
            nc.vector.reciprocal(gs[:, 4:5], gs[:, 3:4]).then_inc(gate_step, 1)
            dve.wait_ge(gate_step, 6)
            nc.vector.tensor_scalar(gp[:], ge[:], gs[:, 4:5], None, ALU.mult).then_inc(gate_step, 1)
            dve.wait_ge(gate_step, 7)
            nc.vector.tensor_reduce(gs[:, 5:6], gp[:], AX.X, ALU.min).then_inc(gate_step, 1)
            dve.wait_ge(gate_step, 8)
            nc.vector.tensor_scalar(gk[:], gp[:], gs[:, 5:6], None, ALU.is_gt).then_inc(gate_step, 1)
            dve.wait_ge(gate_step, 9)
            nc.vector.tensor_tensor(gm[:], gp[:], gk[:], ALU.mult).then_inc(gate_step, 1)
            dve.wait_ge(gate_step, 10)
            nc.vector.tensor_reduce(gs[:, 6:7], gm[:], AX.X, ALU.add).then_inc(gate_step, 1)
            dve.wait_ge(gate_step, 11)
            nc.vector.tensor_scalar(gs[:, 7:8], gs[:, 6:7], 1e-6, None, ALU.max).then_inc(gate_step, 1)
            dve.wait_ge(gate_step, 12)
            nc.vector.reciprocal(gs[:, 3:4], gs[:, 7:8]).then_inc(gate_step, 1)
            dve.wait_ge(gate_step, 13)
            nc.vector.tensor_scalar(gn[:], gm[:], gs[:, 3:4], None, ALU.mult).then_inc(gate_step, 1)
            dve.wait_ge(gate_step, 14)
            nc.vector.tensor_scalar(g_diag[:, 0:T], ident[0:T, 0:T], gn[:, 0:1], None, ALU.mult).then_inc(gd_ready, 1)
            nc.vector.tensor_scalar(g_diag[:, T:HT].rearrange("p (v u b) -> p v u b", v=2, u=3),
                                    ident[0:T, 0:T].rearrange("p (u v b) -> p v u b", u=3, v=2), gn[:, 1:2], None,
                                    ALU.mult).then_inc(gd_ready, 1)

            dve.wait_ge(gb_ready, 1)
            dve.wait_ge(he_ready, NE)
            nc.vector.tensor_tensor(heG, heT, gb[:].rearrange("p (o c) -> p o c", o=1)
                                    .broadcast_to([128, M, HT]), ALU.mult).then_inc(heg_ready, 1)
            dve.wait_ge(a2_ps, 1)
            nc.vector.tensor_copy(clsT[:], bank[A2_BANK][0:EH, 0:2 * T].rearrange("r (k c) -> r k c", k=2)) \
                .then_inc(clsT_ready, 1)
            dve.wait_ge(h1b_ready, 1)
            for t in range(1, G):
                dve.wait_ge(f2_ps, t)
                nc.vector.tensor_tensor(res[:, t, :], bank[F2_BANK[t % 2]][0:T, 0:E], h1b[:, t, :],
                                        ALU.add).then_inc(res_ready, 1)
                if t == 1:
                    dve.wait_ge(cls_ps, 1)
                    nc.vector.tensor_tensor(res[:, 0, :], bank[CLS_BANK][0:T, 0:E], h1[:, 0, :],
                                            ALU.add).then_inc(res_ready, 1)


def value_block(oT, bank, u, s):
    rows = slice(2 * D * s, 2 * D * (s + 1))
    dst = oT[rows, :, :, u * UNIT:(u + 1) * UNIT].rearrange("r p n i -> r i p n")
    src = bank[PV_BANK[u % 2]][rows, 0:4 * SP].rearrange("r (i p s n) -> r i p s n", i=UNIT, p=2, s=SLOTS)[:, :, :, s, :]
    return dst, src


_INS = ['x', 'L0_tok_g1', 'L0_tok_Wp', 'L0_tok_bp', 'L0_tok_g2', 'L0_attn_w_qkv', 'L0_attn_w_out', 'L0_ffn_moe0_W1',
        'L0_ffn_moe0_b1', 'L0_ffn_moe0_W2', 'L0_ffn_moe0_b2', 'L0_ffn_A1_W', 'L0_ffn_A1_b', 'L0_ffn_A2_W',
        'L0_ffn_A2_b', 'L0_ffn_G_W']


def kernel(**inputs):
    import numpy as _np
    import concourse.bacc as _bacc
    from concourse import mybir as _mybir
    from concourse.bass_utils import run_bass_kernel_spmd as _run

    nc = _bacc.Bacc("TRN2", target_bir_lowering=False, num_devices=1)
    arrays, args = {}, []
    for name in _INS:
        a = _np.ascontiguousarray(inputs[name])
        arrays[f"in_{name}_dram"] = a
        args.append(nc.dram_tensor(f"in_{name}_dram", a.shape, _mybir.dt.from_np(a.dtype), kind="ExternalInput").ap())
    args.append(nc.dram_tensor("out_0_dram", (B, N, E), F32, kind="ExternalOutput").ap())
    vit_tower(nc, *args)
    r = _run(nc, [arrays], core_ids=[0])
    return r.results[0]["out_0_dram"]
```

```python
from contextlib import ExitStack

import concourse.bass as bass
from concourse import mybir

F32 = mybir.dt.float32
ALU = mybir.AluOpType
ACT = mybir.ActivationFunctionType
AX = mybir.AxisListType

B, C, IMG, PATCH = 16, 3, 96, 16
G = IMG // PATCH
N = G * G
T = G * B
NTOK = B * N
PD = C * PATCH * PATCH
KT = PD // 128
E = 192
EH = E // 2
HEADS, D = 12, 16
SLOTS = 3
HALF = SLOTS * D
HPAD = 64
QR = HPAD + HALF
SP = SLOTS * N
SC = 2 * N
PR = HPAD + N
F = 768
M = F // 128
NE = 5
NU_E = 3
PPAD = 64
NCLS = 6
RING = 3
UNIT = 2
NU = B // UNIT
CHUNK = 8
EPS_RMS, EPS_LN = 1e-4, 1e-5
PAIRS = G // 2

XT_BANK, EMB_BANK, R1_BANK = (0, 1), (2, 3, 4, 5, 6, 7), 0
LN1_BANK, QK_BANK = (0, 1), (2, 3, 4, 5, 6, 7)
S_BANK, PV_BANK, KP_BANK, PT_BANK = (0, 1), (2, 3), (4, 5), (6, 7)
WO_BANK, LN2_BANK, GATE_BANK = (0, 1, 4, 5), (6, 7), 4
HU_BANK, HV_BANK = (2, 3), (0, 1)
F1_BANK, YU_BANK, YV_BANK, F2_BANK = (4, 5), 6, 7, (2, 3)


def vit_tower(nc: bass.Bass, x, g1, wp, bp, g2, w_qkv, w_out, moe_w1, moe_b1, moe_w2, moe_b2,
              a1_w, a1_b, a2_w, a2_b, g_w, out):
    with ExitStack() as ctx:
        def sb(name, shape):
            return ctx.enter_context(nc.sbuf_tensor(name, shape, F32))

        def sem(name):
            return ctx.enter_context(nc.semaphore(name))

        bank = [ctx.enter_context(nc.psum_tensor(f"bank{i}", [128, 512], F32)) for i in range(8)]

        wp_g = sb("wp_g", [128, KT, E])
        g1_sb = sb("g1_sb", [128, KT])
        bp_bc = sb("bp_bc", [T, E])
        g2_bc = sb("g2_bc", [T, E])
        b2_bc = sb("b2_bc", [T, E])
        wqk = sb("wqk", [EH, 2, 8, HPAD])
        wo = sb("wo", [EH, 2, E])
        w1 = sb("w1", [EH + 1, 2, F])
        w2 = sb("w2", [128, M, E])
        a1 = sb("a1", [EH + 1, NE, 2, F])
        a2 = sb("a2", [128, NE, M, E])
        b2u = sb("b2u", [T, E])
        b2v = sb("b2v", [T, E])
        gw = sb("gw", [EH, 2, NCLS, 2])
        ident = sb("ident", [128, 128])
        ones = sb("ones", [T, 128])
        neg_half = sb("neg_half", [T, G])
        img_mask = sb("img_mask", [T, B])
        row_mask = sb("row_mask", [T, G])
        cls_mask = sb("cls_mask", [T, NCLS])
        slot_mask = sb("slot_mask", [QR, SLOTS])
        x_buf = sb("x_buf", [128, C * PATCH * IMG])
        x_sb = x_buf[0:B * G, :].rearrange("p (c f) -> p c f", c=C)
        xr_buf = sb("xr_buf", [128, C * G * PATCH * PATCH])
        x_r = xr_buf[0:B * G, :].rearrange("p (c w f) -> p c w f", c=C, w=G)
        xT_buf = sb("xT_buf", [128, KT * NTOK])
        xT = xT_buf[:].rearrange("p (k n) -> p k n", k=KT)
        h1 = sb("h1", [T, G, E])
        squares = h1[:].rearrange("p t e -> p (t e)")[:, 0:C * PATCH * PATCH].rearrange(
            "p (c r f) -> p c r f", c=C, r=PATCH)
        ss = sb("ss", [B * G, G])
        ss_diag = sb("ss_diag", [B * G, G, B])
        ms1 = sb("ms1", [T, G])
        r1 = sb("r1", [T, G])
        y = sb("y", [T, G, E])
        y_sq = sb("y_sq", [T, E])
        ms2 = sb("ms2", [T, G])
        ms2e = sb("ms2e", [T, G])
        z = sb("z", [T, G, E])
        r2 = sb("r2", [T, G])
        h0 = sb("h0", [T, G, E])
        stats = sb("stats", [T, 2, G, 6])
        mv = sb("mv", [T, 2, G, 2])
        ve = sb("ve", [T, 2, G])
        rs = sb("rs", [T, 2, G])
        xn = sb("xn", [T, G, E])
        xnT = sb("xnT", [EH, 2, B, N])
        q_bd = xr_buf[0:QR, 0:2 * B * SP].rearrange("r (p b s n) -> r p b s n", p=2, b=B, s=SLOTS)
        k_bd = sb("k_bd", [QR, 2, B, 2, HPAD])
        s_max = sb("s_max", [SP, RING, 8])
        s_sub = sb("s_sub", [SP, RING, 8, N])
        e_sb = sb("e_sb", [SP, RING, 8, N])
        e_sum = sb("e_sum", [SP, RING, 8])
        e_inv = sb("e_inv", [SP, RING, 8])
        p_sb = sb("p_sb", [SP, RING, 8, HPAD])
        pT = sb("pT", [PR, 2, 4, SP])
        kp = sb("kp", [PR, 2, 4, SLOTS, 2, D])
        oT = sb("oT", [EH, 2, N, B])
        h1b = y
        xn2 = z
        x2T = sb("x2T", [EH + 1, 2, NTOK])
        hT = x_buf[:, 0:M * (NTOK - T)].rearrange("p (m n) -> p m n", m=M)
        hid = [xT_buf[:, o:o + n] for o, n in ((0, F), (F, F), (2 * F, M * T), (2 * F + M * T, M * T),
                                               (2 * F + 2 * M * T, M * T))]
        hu, hv = hid[0], hid[1]
        huT = [h.rearrange("r (m c) -> r m c", m=M) for h in hid[2:4]]
        hvT = hid[4].rearrange("r (m c) -> r m c", m=M)
        x2P = sb("x2P", [EH + 1, 2, 2, PPAD])
        hc = sb("hc", [T, 2, E])
        lg6 = sb("lg6", [T, 2, NCLS])
        lg = sb("lg", [T, 2])
        gs = sb("gs", [T, 8])
        ge = sb("ge", [T, 2])
        gp = sb("gp", [T, 2])
        gk = sb("gk", [T, 2])
        gm = sb("gm", [T, 2])
        gn = sb("gn", [T, 2])
        cls_part = sb("cls_part", [T, E])
        res = xn

        x_in = [sem(f"x_in{c}") for c in range(C)]
        wp_in, vec_in, wqk_in, wo_in, w1_in, a1_in, gw_in, w2_in, a2_in = (
            sem(n) for n in ("wp_in", "vec_in", "wqk_in", "wo_in", "w1_in", "a1_in", "gw_in", "w2_in", "a2_in"))
        out_done = sem("out_done")
        consts, wpg_ready, r1_ready, r2_ready, rs_ready, h0_ready, p_ready, h1b_ready, pool_step = (
            sem(n) for n in ("consts", "wpg_ready", "r1_ready", "r2_ready", "rs_ready", "h0_ready", "p_ready", "h1b_ready",
                             "pool_step"))
        xt_ps, r1_ps, emb_ps, ln1_ps, qk_ps, s_ps, kp_ps, pt_ps, pv_ps, wo_ps, ln2_ps, gate_ps, hu_ps, hv_ps, \
            huT_ps, hvT_ps, f1_ps, yu_ps, yv_ps, f2_ps = (
                sem(n) for n in ("xt_ps", "r1_ps", "emb_ps", "ln1_ps", "qk_ps", "s_ps", "kp_ps", "pt_ps", "pv_ps",
                                 "wo_ps", "ln2_ps", "gate_ps", "hu_ps", "hv_ps", "huT_ps", "hvT_ps", "f1_ps",
                                 "yu_ps", "yv_ps", "f2_ps"))
        masks, xr_ready, xt_ready, diag_ready, ms1_ready, y_ready, z_ready, stat_ready, mv_ready, xn_ready, q_ready, max_ready, \
            sub_ready, sum_ready, inv_ready, ov_ready, h1_ready, xn2_ready, gate_step, hc_ready, eT_ready, \
            part_ready, res_ready = (
                sem(n) for n in ("masks", "xr_ready", "xt_ready", "diag_ready", "ms1_ready", "y_ready", "z_ready", "stat_ready",
                                 "mv_ready", "xn_ready", "q_ready", "max_ready", "sub_ready", "sum_ready",
                                 "inv_ready", "ov_ready", "h1_ready", "xn2_ready", "gate_step", "hc_ready",
                                 "eT_ready", "part_ready", "res_ready"))
        ss_ready, ms2_ready, xnT_ready, k_ready, e_ready, pT_ready, kp_ready, oa_ready, x2T_ready, x2P_ready, \
            ge_ready, hu_ready, hv_ready, h_ready = (
                sem(n) for n in ("ss_ready", "ms2_ready", "xnT_ready", "k_ready", "e_ready", "pT_ready", "kp_ready",
                                 "oa_ready", "x2T_ready", "x2P_ready", "ge_ready", "hu_ready", "hv_ready", "h_ready"))

        block = ctx.enter_context(nc.Block())

        @block.sync
        def _(sp):
            x_rows = x.rearrange("b c (h p) w -> c b h (p w)", p=PATCH)
            w_rows = wp.rearrange("(q p c) e -> p q (c e)", q=2, c=C)
            sp.dma_start(x_sb[:, 0, :], x_rows[0]).then_inc(x_in[0], 16)
            sp.dma_start(wp_g[:].rearrange("p (q c) e -> p q (c e)", q=2), w_rows).then_inc(wp_in, 16)
            sp.dma_start(g1_sb[:].rearrange("p (q c) -> p q c", q=2),
                         g1.rearrange("(q p c) -> p q c", q=2, c=C)).then_inc(wp_in, 16)
            for c in range(1, C):
                sp.dma_start(x_sb[:, c, :], x_rows[c]).then_inc(x_in[c], 16)
            for vec, dst in ((bp, bp_bc), (g2, g2_bc), (moe_b2, b2_bc)):
                sp.dma_start(dst[:], vec.rearrange("(o e) -> o e", o=1).broadcast_to([T, E])).then_inc(vec_in, 16)
            for k in range(2):
                sp.dma_start(wqk[:, k, :, 0:HALF], w_qkv[k * EH:(k + 1) * EH, 0:2 * E]
                             .rearrange("r (g f) -> r g f", f=HALF)).then_inc(wqk_in, 16)
            wo_rows = w_out.rearrange("(p g s d) e -> s p g d e", p=2, g=2, s=SLOTS)
            for s in range(SLOTS):
                for p in range(2):
                    sp.dma_start(wo[2 * D * s:2 * D * (s + 1), p, :], wo_rows[s, p]).then_inc(wo_in, 16)
            for k in range(2):
                sp.dma_start(gw[:, k, :, :], g_w[:, k * EH:(k + 1) * EH, :].rearrange("i r g -> r i g")) \
                    .then_inc(gw_in, 16)
            a1_rows = a1_w.rearrange("a (k r) f -> a r k f", k=2)
            for a in range(NE):
                sp.dma_start(a1[0:EH, a, :, :], a1_rows[a]).then_inc(a1_in, 16)
            sp.dma_start(a1[EH:EH + 1, :, 0, :], a1_b.rearrange("(o a) f -> o a f", o=1)).then_inc(a1_in, 16)
            sp.dma_start(w1[0:EH, :, :], moe_w1.rearrange("(k r) f -> r k f", k=2)).then_inc(w1_in, 16)
            sp.dma_start(w1[EH:EH + 1, 0, :], moe_b1.rearrange("(o f) -> o f", o=1)).then_inc(w1_in, 16)
            for u in range(NU_E):
                rows = slice(2 * B * u, 2 * B * (u + 1))
                sp.dma_start(b2u[rows, :], a2_b[u:u + 1, :].broadcast_to([2 * B, E])).then_inc(a2_in, 16)
                for v in range(2):
                    rows = slice(B * (2 * u + v), B * (2 * u + v + 1))
                    sp.dma_start(b2v[rows, :], a2_b[3 + v:4 + v, :].broadcast_to([B, E])).then_inc(a2_in, 16)
            a2_rows = a2_w.rearrange("a (m r) e -> a r m e", m=M)
            for a in range(NE):
                sp.dma_start(a2[:, a, :, :], a2_rows[a]).then_inc(a2_in, 16)
            sp.dma_start(w2[:], moe_w2.rearrange("(m r) e -> r m e", m=M)).then_inc(w2_in, 16)
            out_rows = out.rearrange("b (t w) e -> t w b e", t=G)
            for t in range(G):
                sp.wait_ge(res_ready, t + 1)
                sp.dma_start(out_rows[t], res[:, t, :]).then_inc(out_done, 16)
            sp.wait_ge(out_done, 16 * G)

        @block.gpsimd
        def _(pool):
            nc.gpsimd.memset(ident[:], 0.0).then_inc(pool_step, 1)
            pool.wait_ge(pool_step, 1)
            nc.gpsimd.affine_select(out=ident[:], in_=ident[:], compare_op=ALU.not_equal, fill=1.0, base=0,
                                    pattern=[[-1, 128]], channel_multiplier=1).then_inc(consts, 1)
            pool.wait_ge(wp_in, 32)
            for kt in range(KT):
                k = (kt % 2) * C + kt // 2
                nc.gpsimd.tensor_tensor(wp_g[:, k, :], wp_g[:, k, :], g1_sb[:, k:k + 1].broadcast_to([128, E]),
                                        ALU.mult).then_inc(wpg_ready, 1)
            nc.gpsimd.memset(neg_half[:], -0.5).then_inc(consts, 1)
            nc.gpsimd.memset(ones[:], 1.0).then_inc(consts, 1)
            nc.gpsimd.memset(wqk[:, :, :, HALF:HPAD], 0.0).then_inc(consts, 1)
            nc.gpsimd.memset(p_sb[:], 0.0).then_inc(consts, 1)
            nc.gpsimd.memset(k_bd[:], 0.0).then_inc(consts, 1)
            pool.wait_ge(consts, 6)
            pool.wait_ge(ms1_ready, 1)
            nc.gpsimd.tensor_tensor(r1[:], ms1[:], neg_half[:], ALU.pow).then_inc(r1_ready, 1)
            step = 1

            def small(ins):
                nonlocal step
                ins.then_inc(pool_step, 1)
                step += 1
                pool.wait_ge(pool_step, step)

            def norm1(g):
                cols = slice(2 * g, 2 * g + 2)
                pool.wait_ge(ms2_ready, 2 * g + 2)
                small(nc.gpsimd.tensor_scalar(ms2e[:, cols], ms2[:, cols], 1.0 / E, EPS_RMS, ALU.mult, ALU.add))
                small(nc.gpsimd.tensor_scalar(ve[:, 0, cols], ms2e[:, cols], EPS_LN, None, ALU.mult))
                pool.wait_ge(mv_ready, 2 * g + 2)
                small(nc.gpsimd.tensor_tensor(ve[:, 0, cols], ve[:, 0, cols], mv[:, 0, cols, 1], ALU.add))
                nc.gpsimd.tensor_tensor(rs[:, 0, cols], ve[:, 0, cols], neg_half[:, 0:2], ALU.pow).then_inc(rs_ready, 1)

            def norm2(g):
                cols = slice(2 * g, 2 * g + 2)
                pool.wait_ge(mv_ready, G + 2 * g + 2)
                small(nc.gpsimd.tensor_scalar(ve[:, 1, cols], mv[:, 1, cols, 1], EPS_LN, None, ALU.add))
                nc.gpsimd.tensor_tensor(rs[:, 1, cols], ve[:, 1, cols], neg_half[:, 0:2], ALU.pow).then_inc(rs_ready, 1)

            for g in range(PAIRS):
                norm1(g)
            nc.gpsimd.tensor_tensor(r2[:], ms2e[:], neg_half[:], ALU.pow).then_inc(r2_ready, 1)
            pool.wait_ge(r2_ready, 1)
            nc.gpsimd.tensor_tensor(h0[:], z[:], r2[:].rearrange("p (t o) -> p t o", o=1).broadcast_to([T, G, E]),
                                    ALU.mult).then_inc(h0_ready, 1)
            pool.wait_ge(emb_ps, G)
            for par in range(2):
                nc.gpsimd.memset(huT[par], 0.0).then_inc(consts, 1)
            for u in range(NU):
                pool.wait_ge(inv_ready, u + 1)
                if u >= RING:
                    pool.wait_ge(pt_ps, u - RING + 1)
                nc.gpsimd.tensor_tensor(p_sb[:, u % RING, :, 0:N], e_sb[:, u % RING, :, :],
                                        e_inv[:, u % RING, :].rearrange("p (k o) -> p k o", o=1)
                                        .broadcast_to([SP, 8, N]), ALU.mult).then_inc(p_ready, 1)
            for g in range(PAIRS):
                norm2(g)
            pool.wait_ge(vec_in, 48)
            pool.wait_ge(h1_ready, G)
            nc.gpsimd.tensor_tensor(h1b[:, 1:G, :], h1[:, 1:G, :], b2_bc[:].rearrange("p (o e) -> p o e", o=1)
                                    .broadcast_to([T, G - 1, E]), ALU.add).then_inc(h1b_ready, 1)

        @block.tensor
        def _(pe):
            pe.wait_ge(consts, 1)

            def transpose_patches(kt):
                c, q = kt // 2, kt % 2
                if q == 0:
                    pe.wait_ge(xr_ready, c + 1)
                for half in range(2):
                    f = 2 * kt + half
                    if f >= 2:
                        pe.wait_ge(xt_ready, f - 1)
                    for w in range(3):
                        last = nc.tensor.transpose(bank[XT_BANK[f % 2]][:, w * T:(w + 1) * T], x_r[:, c, 3 * half + w, q * 128:(q + 1) * 128],
                                                   ident[0:T, 0:T])
                    last.then_inc(xt_ps, 1)

            def embed(kt, t):
                return nc.tensor.matmul(bank[EMB_BANK[t]][0:T, 0:E], xT[:, kt, t * T:(t + 1) * T],
                                        wp_g[:, (kt % 2) * C + kt // 2, :], start=(kt == 0), stop=(kt == KT - 1))

            def embed_all(kt):
                pe.wait_ge(xt_ready, 2 * kt + 2)
                pe.wait_ge(wpg_ready, kt + 1)
                for t in range(G):
                    embed(kt, t)

            transpose_patches(0)
            transpose_patches(1)
            for kt in range(KT - 3):
                embed_all(kt)
                transpose_patches(kt + 2)
            transpose_patches(KT - 1)
            pe.wait_ge(xt_ready, 2 * KT - 1)
            pe.wait_ge(diag_ready, 1)
            nc.tensor.matmul(bank[R1_BANK][0:T, 0:G], ss_diag[:].rearrange("p w b -> p (w b)"), row_mask[:],
                             start=True, stop=True).then_inc(r1_ps, 1)
            embed_all(KT - 3)
            pe.wait_ge(xt_ready, 2 * KT)
            pe.wait_ge(wpg_ready, KT)
            for t in range(G):
                embed(KT - 2, t)
                embed(KT - 1, t).then_inc(emb_ps, 1)

            for t in range(G):
                pe.wait_ge(xn_ready, t + 1)
                if t == 0:
                    pe.wait_ge(ms1_ready, 1)
                if t >= 2:
                    pe.wait_ge(xnT_ready, t - 1)
                for k in range(2):
                    last = nc.tensor.transpose(bank[LN1_BANK[t % 2]][0:EH, k * T:(k + 1) * T],
                                               xn[:, t, k * EH:(k + 1) * EH], ident[0:T, 0:T])
                last.then_inc(ln1_ps, 1)

            def project(ch):
                for s in range(4):
                    o = 4 * ch + s
                    if o >= len(QK_BANK):
                        pe.wait_ge(q_ready, o - len(QK_BANK) + 1)
                    for k in range(2):
                        last = nc.tensor.matmul(
                            bank[QK_BANK[o % len(QK_BANK)]][0:QR, 0:CHUNK * N],
                            wqk[:, k, 2 * s:2 * s + 2, :].rearrange("r g f -> r (g f)")[:, 0:QR],
                            xnT[:, k, ch * CHUNK:(ch + 1) * CHUNK, :].rearrange("r b n -> r (b n)"),
                            start=(k == 0), stop=(k == 1))
                    last.then_inc(qk_ps, 1)

            pe.wait_ge(xnT_ready, G)
            pe.wait_ge(wqk_in, 32)
            pe.wait_ge(consts, 6)

            def scores(u):
                ch = u * UNIT // CHUNK
                pe.wait_ge(q_ready, 2 * (ch + 1))
                pe.wait_ge(k_ready, 4 * (ch + 1))
                if u >= 2:
                    pe.wait_ge(sub_ready, u - 1)
                for i in range(UNIT):
                    for p in range(2):
                        n = 2 * i + p
                        last = nc.tensor.matmul(bank[S_BANK[u % 2]][0:SP, n * SC:(n + 1) * SC],
                                                q_bd[:, p, u * UNIT + i, :, :].rearrange("r s n -> r (s n)"),
                                                k_bd[:, p, u * UNIT + i, :, 0:N], start=True, stop=True)
                last.then_inc(s_ps, 1)

            def keys(u):
                pe.wait_ge(k_ready, 4 * (u * UNIT // CHUNK + 1))
                if u >= 2:
                    pe.wait_ge(kp_ready, 2 * (u - 1))
                for i in range(UNIT):
                    for p in range(2):
                        n = 2 * i + p
                        last = nc.tensor.transpose(
                            bank[KP_BANK[u % 2]][0:PR, n * QR:(n + 1) * QR],
                            k_bd[:, p, u * UNIT + i, :, :].rearrange("r g j -> r (g j)")[:, 0:PR], ident[0:QR, 0:QR])
                last.then_inc(kp_ps, 1)

            def probs(u):
                pe.wait_ge(p_ready, u + 1)
                if u == 0:
                    pe.wait_ge(q_ready, 4)
                if u >= 2:
                    pe.wait_ge(pT_ready, u - 1)
                for n in range(2 * UNIT):
                    last = nc.tensor.transpose(
                        bank[PT_BANK[u % 2]][0:PR, n * SP:(n + 1) * SP],
                        p_sb[:, u % RING, 2 * n:2 * n + 2, :].rearrange("r g j -> r (g j)")[:, 0:PR], ident[0:SP, 0:SP])
                last.then_inc(pt_ps, 1)

            def values(u):
                pe.wait_ge(pT_ready, u + 1)
                pe.wait_ge(kp_ready, 2 * (u + 1))
                if u == 0:
                    pe.wait_ge(k_ready, 8)
                if u >= 2:
                    pe.wait_ge(ov_ready, 2 * (u - 1))
                    pe.wait_ge(oa_ready, u - 1)
                for n in range(2 * UNIT):
                    last = nc.tensor.matmul(bank[PV_BANK[u % 2]][0:EH, n * SP:(n + 1) * SP],
                                            kp[:, u % 2, n].rearrange("r s g d -> r (s g d)"),
                                            pT[:, u % 2, n, :], start=True, stop=True)
                last.then_inc(pv_ps, 1)

            project(0)
            scores(0)
            scores(1)
            keys(0)
            project(1)
            scores(2)
            for u in range(NU):
                probs(u)
                if u + RING < NU:
                    scores(u + RING)
                if u + 1 < NU:
                    keys(u + 1)
                values(u)

            pe.wait_ge(ov_ready, 2 * NU)
            pe.wait_ge(oa_ready, NU)
            pe.wait_ge(wo_in, 96)
            for t in range(G):
                if t >= len(WO_BANK):
                    pe.wait_ge(h1_ready, t - len(WO_BANK) + 1)
                for p in range(2):
                    last = nc.tensor.matmul(bank[WO_BANK[t % len(WO_BANK)]][0:T, 0:E],
                                            oT[:, p, t * G:(t + 1) * G, :].rearrange("r n b -> r (n b)"),
                                            wo[:, p, :], start=(p == 0), stop=(p == 1))
                last.then_inc(wo_ps, 1)

            def transpose_ln2(t):
                pe.wait_ge(xn2_ready, t + 1)
                if t >= 2:
                    pe.wait_ge(x2T_ready, t - 1)
                    pe.wait_ge(x2P_ready, 2)
                for k in range(2):
                    last = nc.tensor.transpose(bank[LN2_BANK[t % 2]][0:EH, k * T:(k + 1) * T],
                                               xn2[:, t, k * EH:(k + 1) * EH], ident[0:T, 0:T])
                last.then_inc(ln2_ps, 1)

            def hidden_u():
                pe.wait_ge(a1_in, 16 * (NE + 1))
                for j, cols in enumerate((slice(0, 512), slice(512, F))):
                    for k in range(2):
                        rows = EH + 1 - k
                        for u in range(NU_E):
                            tok = slice(2 * B * u, 2 * B * (u + 1))
                            last = nc.tensor.matmul(bank[HU_BANK[j]][tok, 0:cols.stop - cols.start], x2T[0:rows, k, tok],
                                                    a1[0:rows, u, k, cols], start=(k == 0), stop=(k == 1))
                    last.then_inc(hu_ps, 1)

            def hidden_v():
                pe.wait_ge(x2P_ready, 2)
                pe.wait_ge(h1_ready, G)
                for j, cols in enumerate((slice(0, 512), slice(512, F))):
                    for k in range(2):
                        rows = EH + 1 - k
                        for v in range(2):
                            last = nc.tensor.matmul(
                                bank[HV_BANK[j]][PPAD * v:PPAD * (v + 1), 0:cols.stop - cols.start],
                                x2P[0:rows, k, v, :], a1[0:rows, 3 + v, k, cols], start=(k == 0), stop=(k == 1))
                    last.then_inc(hv_ps, 1)

            def transpose_hidden(src, rows, banks, done):
                for j in range(2):
                    for i in range(3):
                        m = 3 * j + i
                        last = nc.tensor.transpose(bank[banks[j]][:, i * rows:(i + 1) * rows],
                                                   src[0:rows, m * 128:(m + 1) * 128], ident[0:rows, 0:rows])
                    last.then_inc(done, 1)

            def patch_hidden(m):
                if m >= 2:
                    pe.wait_ge(h_ready, m - 1)
                for k in range(2):
                    rows = EH + 1 - k
                    last = nc.tensor.matmul(bank[F1_BANK[m % 2]][:, 0:NTOK - T], w1[0:rows, k, m * 128:(m + 1) * 128],
                                            x2T[0:rows, k, T:NTOK], start=(k == 0), stop=(k == 1))
                last.then_inc(f1_ps, 1)

            transpose_ln2(0)
            pe.wait_ge(x2T_ready, 1)
            pe.wait_ge(gw_in, 32)
            pe.wait_ge(masks, 7)
            pe.wait_ge(h1_ready, 4)
            for k in range(2):
                last = nc.tensor.matmul(bank[GATE_BANK][0:T, 0:2 * NCLS], x2T[0:EH, k, 0:T],
                                        gw[:, k, :, :].rearrange("r i g -> r (i g)"), start=(k == 0), stop=(k == 1))
            last.then_inc(gate_ps, 1)
            hidden_u()
            transpose_ln2(1)
            hidden_v()
            for t in range(2, G):
                transpose_ln2(t)
            pe.wait_ge(x2T_ready, G)
            pe.wait_ge(w1_in, 32)
            pe.wait_ge(gate_step, 1)
            patch_hidden(0)
            patch_hidden(1)
            pe.wait_ge(hu_ready, 2)
            transpose_hidden(hu, T, HU_BANK, huT_ps)
            patch_hidden(2)
            pe.wait_ge(hv_ready, 2)
            transpose_hidden(hv, 2 * PPAD, HV_BANK, hvT_ps)
            for m in range(3, M):
                patch_hidden(m)
            pe.wait_ge(eT_ready, 8)
            pe.wait_ge(a2_in, 16 * (3 * NU_E + NE))
            for v in range(2):
                for m in range(M):
                    last = nc.tensor.matmul(bank[YU_BANK][0:T, 0:E], huT[v][:, m, :], a2[:, 3 + v, m, :],
                                            start=(v == 0 and m == 0), stop=(v == 1 and m == M - 1))
            last.then_inc(yu_ps, 1)
            for m in range(M):
                for u in range(NU_E):
                    tok = slice(2 * B * u, 2 * B * (u + 1))
                    last = nc.tensor.matmul(bank[YV_BANK][tok, 0:E], hvT[:, m, tok], a2[:, u, m, :],
                                            start=(m == 0), stop=(m == M - 1))
            last.then_inc(yv_ps, 1)
            pe.wait_ge(h_ready, M)
            pe.wait_ge(w2_in, 16)
            for t in range(1, G):
                if t >= 3:
                    pe.wait_ge(res_ready, t - 1)
                for m in range(M):
                    last = nc.tensor.matmul(bank[F2_BANK[t % 2]][0:T, 0:E], hT[:, m, (t - 1) * T:t * T], w2[:, m, :],
                                            start=(m == 0), stop=(m == M - 1))
                last.then_inc(f2_ps, 1)

        @block.scalar
        def _(act):
            for c in range(C):
                act.wait_ge(x_in[c], 16)
            patches = x_sb.rearrange("p c (r w f) -> p w c r f", r=PATCH, w=G)
            for w in range(G):
                if w >= 1:
                    act.wait_ge(ss_ready, w)
                nc.scalar.activation(squares, patches[:, w], ACT.Square,
                                     accum_out=ss[:, w:w + 1]).then_inc(ss_ready, 1)
            for t in range(G):
                act.wait_ge(y_ready, t + 1)
                if t >= 1:
                    act.wait_ge(ms2_ready, t)
                nc.scalar.activation(y_sq[:], y[:, t, :], ACT.Square, accum_out=ms2[:, t:t + 1]).then_inc(ms2_ready, 1)
            for t in range(G):
                act.wait_ge(ln1_ps, t + 1)
                nc.scalar.activation(xnT[:, :, :, t * G:(t + 1) * G].rearrange("r k b n -> r k n b"),
                                     bank[LN1_BANK[t % 2]][0:EH, 0:2 * T].rearrange("r (k n b) -> r k n b", k=2, n=G),
                                     ACT.Copy).then_inc(xnT_ready, 1)
            def take_k(ch):
                for p in range(2):
                    o = 4 * ch + 2 + p
                    act.wait_ge(qk_ps, o + 1)
                    src = bank[QK_BANK[o % len(QK_BANK)]]
                    for hg in range(2):
                        rows = slice(hg * HPAD, hg * HPAD + HALF)
                        nc.scalar.activation(k_bd[rows, p, ch * CHUNK:(ch + 1) * CHUNK, hg, 0:N],
                                             src[rows, 0:CHUNK * N].rearrange("r (b n) -> r b n", b=CHUNK),
                                             ACT.Copy).then_inc(k_ready, 1)

            def exponentials(u):
                act.wait_ge(sub_ready, u + 1)
                if u >= RING:
                    act.wait_ge(p_ready, u - RING + 1)
                    act.wait_ge(sum_ready, u - RING + 1)
                nc.scalar.activation(e_sb[:, u % RING, :, :], s_sub[:, u % RING, :, :], ACT.Exp,
                                     scale=float(E) ** -0.5).then_inc(e_ready, 1)

            def copy_keys(u):
                act.wait_ge(kp_ps, u + 1)
                if u >= 2:
                    act.wait_ge(pv_ps, u - 1)
                src = bank[KP_BANK[u % 2]][0:PR, 0:4 * QR].rearrange("r (n c) -> r n c", n=4)
                for hg in range(2):
                    nc.scalar.activation(kp[:, u % 2, :, :, hg, :], src[:, :, hg * HPAD:hg * HPAD + HALF]
                                         .rearrange("r n (s d) -> r n s d", s=SLOTS), ACT.Copy).then_inc(kp_ready, 1)

            def copy_probs(u):
                act.wait_ge(pt_ps, u + 1)
                if u >= 2:
                    act.wait_ge(pv_ps, u - 1)
                nc.scalar.activation(pT[:, u % 2, :, :], bank[PT_BANK[u % 2]][0:PR, 0:4 * SP]
                                     .rearrange("r (n c) -> r n c", n=4), ACT.Copy).then_inc(pT_ready, 1)

            def take_values(u):
                act.wait_ge(pv_ps, u + 1)
                nc.scalar.activation(*value_block(oT, bank, u, 0), ACT.Copy).then_inc(oa_ready, 1)

            act.wait_ge(consts, 6)
            take_k(0)
            exponentials(0)
            copy_keys(0)
            exponentials(1)
            take_k(1)
            exponentials(2)
            for u in range(NU):
                copy_probs(u)
                if u + RING < NU:
                    exponentials(u + RING)
                if u + 1 < NU:
                    copy_keys(u + 1)
                take_values(u)

            def copy_ln2(t):
                act.wait_ge(ln2_ps, t + 1)
                nc.scalar.activation(x2T[0:EH, :, t * T:(t + 1) * T],
                                     bank[LN2_BANK[t % 2]][0:EH, 0:2 * T].rearrange("r (k c) -> r k c", k=2),
                                     ACT.Copy).then_inc(x2T_ready, 1)

            copy_ln2(0)
            for k in range(2):
                nc.scalar.activation(x2P[0:EH, k, :, 0:PPAD - B].rearrange("r v (u b) -> r v u b", u=NU_E),
                                     bank[LN2_BANK[0]][0:EH, k * T:(k + 1) * T]
                                     .rearrange("r (u v b) -> r v u b", u=NU_E, v=2), ACT.Copy).then_inc(x2P_ready, 1)
            for t in range(1, G):
                copy_ln2(t)
            act.wait_ge(gate_step, 4)
            nc.scalar.activation(ge[:], gs[:, 1:3], ACT.Exp).then_inc(ge_ready, 1)
            for dst, rows, banks, done, ready in ((hu, T, HU_BANK, hu_ps, hu_ready),
                                                  (hv, 2 * PPAD, HV_BANK, hv_ps, hv_ready)):
                for j, (a, b) in enumerate(((0, 512), (512, F))):
                    act.wait_ge(done, j + 1)
                    nc.scalar.activation(dst[0:rows, a:b], bank[banks[j]][0:rows, 0:b - a], ACT.Gelu) \
                        .then_inc(ready, 1)
            for m in range(M):
                act.wait_ge(f1_ps, m + 1)
                nc.scalar.activation(hT[:, m, :], bank[F1_BANK[m % 2]][:, 0:NTOK - T], ACT.Gelu).then_inc(h_ready, 1)

        @block.vector
        def _(dve):
            dve.wait_ge(consts, 1)
            nc.vector.tensor_reduce(img_mask[:], ident[0:T, 0:T].rearrange("p (b h) -> p b h", b=B), AX.X,
                                    ALU.add).then_inc(masks, 1)
            nc.vector.tensor_reduce(row_mask[:], ident[0:T, 0:T].rearrange("p (b h) -> p h b", b=B), AX.X,
                                    ALU.add).then_inc(masks, 1)
            nc.vector.tensor_reduce(cls_mask[:], ident[0:T, 0:T].rearrange("p (i b) -> p i b", i=NCLS), AX.X,
                                    ALU.add).then_inc(masks, 1)
            nc.vector.tensor_reduce(
                slot_mask[:], ident[0:QR, :].rearrange("p (g f) -> p g f", g=2)[:, :, 0:HALF]
                .rearrange("p g (s d) -> p s g d", s=SLOTS), AX.XY, ALU.add).then_inc(masks, 1)
            nc.vector.memset(x2T[EH:EH + 1, 0, :], 1.0).then_inc(masks, 1)
            nc.vector.memset(x2P[EH:EH + 1, 0, :, :], 1.0).then_inc(masks, 1)
            nc.vector.memset(x2P[0:EH, :, :, PPAD - B:PPAD], 0.0).then_inc(masks, 1)

            def regroup(c):
                dve.wait_ge(x_in[c], 16)
                nc.vector.tensor_copy(x_r[:, c, :, :].rearrange("p w (r f) -> p w r f", r=PATCH),
                                      x_sb[:, c, :].rearrange("p (r w f) -> p w r f", r=PATCH, w=G)) \
                    .then_inc(xr_ready, 1)

            def spread_sums():
                dve.wait_ge(ss_ready, G)
                dve.wait_ge(masks, 4)
                nc.vector.tensor_tensor(ss_diag[:], ss[:].rearrange("p (w o) -> p w o", o=1).broadcast_to([T, G, B]),
                                        img_mask[:].rearrange("p (o b) -> p o b", o=1).broadcast_to([T, G, B]),
                                        ALU.mult).then_inc(diag_ready, 1)

            regroup(0)
            for f in range(2 * KT):
                if f == 10:
                    spread_sums()
                if f in (1, 3):
                    regroup(f // 2 + 1)
                kt, half = f // 2, f % 2
                dve.wait_ge(xt_ps, f + 1)
                nc.vector.tensor_copy(
                    xT[:, kt, :].rearrange("r (h w b) -> r w b h", h=G, w=G)[:, 3 * half:3 * half + 3],
                    bank[XT_BANK[f % 2]][:, 0:3 * T].rearrange("r (w b h) -> r w b h", w=3, b=B)).then_inc(xt_ready, 1)

            dve.wait_ge(r1_ps, 1)
            nc.vector.tensor_scalar(ms1[:], bank[R1_BANK][0:T, 0:G], 1.0 / PD, EPS_RMS, ALU.mult,
                                    ALU.add).then_inc(ms1_ready, 1)
            dve.wait_ge(vec_in, 48)

            def embedded(g):
                for t in (2 * g, 2 * g + 1):
                    dve.wait_ge(emb_ps, t + 1)
                    if t == 0:
                        dve.wait_ge(r1_ready, 1)
                    nc.vector.scalar_tensor_tensor(out=y[:, t, :], in0=bank[EMB_BANK[t]][0:T, 0:E],
                                                   scalar=r1[:, t:t + 1], in1=bp_bc[:], op0=ALU.mult,
                                                   op1=ALU.add).then_inc(y_ready, 1)

            def statistics(w, h, t, ready):
                dve.wait_ge(ready, t + 1)
                nc.vector.bn_stats(stats[:, w, t, :], h[:, t, :]).then_inc(stat_ready, 1)

            def moments(w, t):
                dve.wait_ge(stat_ready, G * w + t + 1)
                nc.vector.bn_aggr(mv[:, w, t, :], stats[:, w, t, :]).then_inc(mv_ready, 1)

            def normalise(w, h, dst, g, ready):
                dve.wait_ge(rs_ready, PAIRS * w + g + 1)
                for t in (2 * g, 2 * g + 1):
                    nc.vector.tensor_scalar(dst[:, t, :], h[:, t, :], mv[:, w, t, 0:1], rs[:, w, t:t + 1],
                                            ALU.subtract, ALU.mult).then_inc(ready, 1)

            def token_pair(g):
                embedded(g)
                for t in (2 * g, 2 * g + 1):
                    dve.wait_ge(y_ready, t + 1)
                    nc.vector.tensor_tensor(z[:, t, :], y[:, t, :], g2_bc[:], ALU.mult).then_inc(z_ready, 1)
                for t in (2 * g, 2 * g + 1):
                    statistics(0, z, t, z_ready)
                for t in (2 * g, 2 * g + 1):
                    moments(0, t)

            token_pair(0)
            token_pair(1)
            normalise(0, z, xn, 0, xn_ready)
            token_pair(2)
            normalise(0, z, xn, 1, xn_ready)
            normalise(0, z, xn, 2, xn_ready)

            def take_q(o, p, ch):
                dve.wait_ge(qk_ps, o + 1)
                nc.vector.tensor_tensor(
                    q_bd[:, p, ch * CHUNK:(ch + 1) * CHUNK, :, :],
                    bank[QK_BANK[o % len(QK_BANK)]][0:QR, 0:CHUNK * N].rearrange("r (b o n) -> r b o n", b=CHUNK, o=1)
                    .broadcast_to([QR, CHUNK, SLOTS, N]),
                    slot_mask[:].rearrange("r (o s q) -> r o s q", o=1, q=1)
                    .broadcast_to([QR, CHUNK, SLOTS, N]), ALU.mult).then_inc(q_ready, 1)

            def row_max(u):
                dve.wait_ge(s_ps, u + 1)
                s = bank[S_BANK[u % 2]][0:SP, 0:8 * N].rearrange("p (k j) -> p k j", k=8)
                if u >= RING:
                    dve.wait_ge(sub_ready, u - RING + 1)
                nc.vector.tensor_reduce(s_max[:, u % RING, :], s, AX.X, ALU.max).then_inc(max_ready, 1)

            def subtract_max(u):
                dve.wait_ge(max_ready, u + 1)
                if u >= RING:
                    dve.wait_ge(e_ready, u - RING + 1)
                s = bank[S_BANK[u % 2]][0:SP, 0:8 * N].rearrange("p (k j) -> p k j", k=8)
                nc.vector.tensor_tensor(s_sub[:, u % RING, :, :], s, s_max[:, u % RING, :]
                                        .rearrange("p (k o) -> p k o", o=1).broadcast_to([SP, 8, N]),
                                        ALU.subtract).then_inc(sub_ready, 1)

            def row_sum(u):
                dve.wait_ge(e_ready, u + 1)
                if u >= RING:
                    dve.wait_ge(inv_ready, u - RING + 1)
                nc.vector.tensor_reduce(e_sum[:, u % RING, :], e_sb[:, u % RING, :, :], AX.X, ALU.add).then_inc(sum_ready, 1)

            def invert_sum(u):
                dve.wait_ge(sum_ready, u + 1)
                if u >= RING:
                    dve.wait_ge(p_ready, u - RING + 1)
                nc.vector.reciprocal(e_inv[:, u % RING, :], e_sum[:, u % RING, :]).then_inc(inv_ready, 1)

            def take_values(u):
                dve.wait_ge(pv_ps, u + 1)
                for s in (1, 2):
                    dst, src = value_block(oT, bank, u, s)
                    nc.vector.tensor_copy(dst, src).then_inc(ov_ready, 1)

            def shift(u):
                row_max(u)
                subtract_max(u)

            def sums(u):
                row_sum(u)
                invert_sum(u)

            take_q(0, 0, 0)
            take_q(1, 1, 0)
            shift(0)
            shift(1)
            take_q(4, 0, 1)
            sums(0)
            take_q(5, 1, 1)
            sums(1)
            shift(2)
            for u in range(NU):
                if u + RING < NU:
                    shift(u + RING)
                if u + 2 < NU:
                    sums(u + 2)
                take_values(u)

            dve.wait_ge(h0_ready, 1)

            def residual(g):
                for t in (2 * g, 2 * g + 1):
                    dve.wait_ge(wo_ps, t + 1)
                    nc.vector.tensor_tensor(h1[:, t, :], bank[WO_BANK[t % len(WO_BANK)]][0:T, 0:E], h0[:, t, :],
                                            ALU.add).then_inc(h1_ready, 1)
                for t in (2 * g, 2 * g + 1):
                    statistics(1, h1, t, h1_ready)
                for t in (2 * g, 2 * g + 1):
                    moments(1, t)

            residual(0)
            residual(1)
            normalise(1, h1, xn2, 0, xn2_ready)
            residual(2)
            normalise(1, h1, xn2, 1, xn2_ready)
            normalise(1, h1, xn2, 2, xn2_ready)

            dve.wait_ge(gate_ps, 1)
            nc.vector.tensor_tensor(lg6[:], bank[GATE_BANK][0:T, 0:2 * NCLS].rearrange("p (i g) -> p g i", g=2),
                                    cls_mask[:].rearrange("p (o i) -> p o i", o=1).broadcast_to([T, 2, NCLS]),
                                    ALU.mult).then_inc(gate_step, 1)
            dve.wait_ge(gate_step, 1)
            nc.vector.tensor_reduce(lg[:], lg6[:], AX.X, ALU.add).then_inc(gate_step, 1)
            dve.wait_ge(gate_step, 2)
            nc.vector.tensor_reduce(gs[:, 0:1], lg[:], AX.X, ALU.max).then_inc(gate_step, 1)
            dve.wait_ge(gate_step, 3)
            nc.vector.tensor_scalar(gs[:, 1:3], lg[:], gs[:, 0:1], None, ALU.subtract).then_inc(gate_step, 1)
            dve.wait_ge(ge_ready, 1)
            nc.vector.tensor_reduce(gs[:, 3:4], ge[:], AX.X, ALU.add).then_inc(gate_step, 1)
            dve.wait_ge(gate_step, 5)
            nc.vector.reciprocal(gs[:, 4:5], gs[:, 3:4]).then_inc(gate_step, 1)
            dve.wait_ge(gate_step, 6)
            nc.vector.tensor_scalar(gp[:], ge[:], gs[:, 4:5], None, ALU.mult).then_inc(gate_step, 1)
            dve.wait_ge(gate_step, 7)
            nc.vector.tensor_reduce(gs[:, 5:6], gp[:], AX.X, ALU.min).then_inc(gate_step, 1)
            dve.wait_ge(gate_step, 8)
            nc.vector.tensor_scalar(gk[:], gp[:], gs[:, 5:6], None, ALU.is_gt).then_inc(gate_step, 1)
            dve.wait_ge(gate_step, 9)
            nc.vector.tensor_tensor(gm[:], gp[:], gk[:], ALU.mult).then_inc(gate_step, 1)
            dve.wait_ge(gate_step, 10)
            nc.vector.tensor_reduce(gs[:, 6:7], gm[:], AX.X, ALU.add).then_inc(gate_step, 1)
            dve.wait_ge(gate_step, 11)
            nc.vector.tensor_scalar(gs[:, 7:8], gs[:, 6:7], 1e-6, None, ALU.max).then_inc(gate_step, 1)
            dve.wait_ge(gate_step, 12)
            nc.vector.reciprocal(gs[:, 3:4], gs[:, 7:8]).then_inc(gate_step, 1)
            dve.wait_ge(gate_step, 13)
            nc.vector.tensor_scalar(gn[:], gm[:], gs[:, 3:4], None, ALU.mult).then_inc(gate_step, 1)
            dve.wait_ge(gate_step, 14)
            dve.wait_ge(a2_in, 16 * (3 * NU_E + NE))
            nc.vector.scalar_tensor_tensor(out=hc[:, 0, :], in0=b2v[:], scalar=gn[:, 0:1], in1=h1[:, 0, :],
                                           op0=ALU.mult, op1=ALU.add).then_inc(hc_ready, 1)
            dve.wait_ge(hc_ready, 1)
            nc.vector.scalar_tensor_tensor(out=hc[:, 1, :], in0=b2u[:], scalar=gn[:, 1:2], in1=hc[:, 0, :],
                                           op0=ALU.mult, op1=ALU.add).then_inc(hc_ready, 1)
            dve.wait_ge(consts, 8)
            for j in range(2):
                dve.wait_ge(huT_ps, j + 1)
                for v in range(2):
                    nc.vector.tensor_copy(
                        huT[v][:, 3 * j:3 * j + 3, :].rearrange("r m (u v b) -> r m u v b", u=NU_E, v=2)[:, :, :, v, :],
                        bank[HU_BANK[j]][:, 0:3 * T].rearrange("r (m u v b) -> r m u v b", m=3, u=NU_E, v=2)
                        [:, :, :, v, :]).then_inc(eT_ready, 1)
            for j in range(2):
                dve.wait_ge(hvT_ps, j + 1)
                for v in range(2):
                    nc.vector.tensor_copy(
                        hvT[:, 3 * j:3 * j + 3, :].rearrange("r m (u v b) -> r m u v b", u=NU_E, v=2)[:, :, :, v, :],
                        bank[HV_BANK[j]][:, 0:6 * PPAD].rearrange("r (m v c) -> r m v c", m=3, v=2)
                        [:, :, v, 0:PPAD - B].rearrange("r m (u b) -> r m u b", u=NU_E)).then_inc(eT_ready, 1)
            dve.wait_ge(yu_ps, 1)
            dve.wait_ge(hc_ready, 2)
            nc.vector.scalar_tensor_tensor(out=cls_part[:], in0=bank[YU_BANK][0:T, 0:E], scalar=gn[:, 0:1],
                                           in1=hc[:, 1, :], op0=ALU.mult, op1=ALU.add).then_inc(part_ready, 1)
            dve.wait_ge(yv_ps, 1)
            dve.wait_ge(part_ready, 1)
            nc.vector.scalar_tensor_tensor(out=res[:, 0, :], in0=bank[YV_BANK][0:T, 0:E], scalar=gn[:, 1:2],
                                           in1=cls_part[:], op0=ALU.mult, op1=ALU.add).then_inc(res_ready, 1)
            dve.wait_ge(h1b_ready, 1)
            for t in range(1, G):
                dve.wait_ge(f2_ps, t)
                nc.vector.tensor_tensor(res[:, t, :], bank[F2_BANK[t % 2]][0:T, 0:E], h1b[:, t, :],
                                        ALU.add).then_inc(res_ready, 1)


def value_block(oT, bank, u, s):
    rows = slice(2 * D * s, 2 * D * (s + 1))
    dst = oT[rows, :, :, u * UNIT:(u + 1) * UNIT].rearrange("r p n i -> r i p n")
    src = bank[PV_BANK[u % 2]][rows, 0:4 * SP].rearrange("r (i p s n) -> r i p s n", i=UNIT, p=2, s=SLOTS)[:, :, :, s, :]
    return dst, src


_INS = ['x', 'L0_tok_g1', 'L0_tok_Wp', 'L0_tok_bp', 'L0_tok_g2', 'L0_attn_w_qkv', 'L0_attn_w_out', 'L0_ffn_moe0_W1',
        'L0_ffn_moe0_b1', 'L0_ffn_moe0_W2', 'L0_ffn_moe0_b2', 'L0_ffn_A1_W', 'L0_ffn_A1_b', 'L0_ffn_A2_W',
        'L0_ffn_A2_b', 'L0_ffn_G_W']


def kernel(**inputs):
    import numpy as _np
    import concourse.bacc as _bacc
    from concourse import mybir as _mybir
    from concourse.bass_utils import run_bass_kernel_spmd as _run

    nc = _bacc.Bacc("TRN2", target_bir_lowering=False, num_devices=1)
    arrays, args = {}, []
    for name in _INS:
        a = _np.ascontiguousarray(inputs[name])
        arrays[f"in_{name}_dram"] = a
        args.append(nc.dram_tensor(f"in_{name}_dram", a.shape, _mybir.dt.from_np(a.dtype), kind="ExternalInput").ap())
    args.append(nc.dram_tensor("out_0_dram", (B, N, E), F32, kind="ExternalOutput").ap())
    vit_tower(nc, *args)
    r = _run(nc, [arrays], core_ids=[0])
    return r.results[0]["out_0_dram"]
```

```python
from contextlib import ExitStack

import concourse.bass as bass
from concourse import mybir

F32, F32R = mybir.dt.float32, mybir.dt.float32r
ALU = mybir.AluOpType
ACT = mybir.ActivationFunctionType
AX = mybir.AxisListType

B, C, IMG, PATCH = 16, 3, 96, 16
G = IMG // PATCH
N = G * G
NCLS = 6
T = NCLS * B
NTOK = B * N
P = 128
TN = (0, 6, 14, 22, 30, N)
NT = len(TN) - 1
ROWS = tuple((TN[t + 1] - TN[t]) * B for t in range(NT))
PD = C * PATCH * PATCH
KT = PD // 128
E = 192
EH = E // 2
HEADS, D = 12, 16
SLOTS = 3
HALF = SLOTS * D
HPAD = 64
QR = HPAD + HALF
SP = SLOTS * N
SC = 2 * N
PR = HPAD + N
F = 768
M = F // 128
NE = 5
NU_E = 3
PPAD = 64
RING = 3
W1_STEPS = 6
UNIT = 2
NU = B // UNIT
CHUNK = 8
EPS_RMS, EPS_LN = 1e-4, 1e-5
HALVES = ((512, F), (0, 512))
GROUPS1 = ((0, 2), (2, 4), (4, 5))
GROUPS2 = ((0, 1), (1, 3), (3, 5))

XT_BANK, R1_BANK, EMB_BANK = (0, 1), 2, (3, 4, 5, 6, 7)
LN1_BANK, QK_BANK = (0, 1, 5, 6, 7), (2, 3, 4, 5, 6, 7)
S_BANK, PV_BANK, KP_BANK, PT_BANK = (0, 1), (2, 3), (4, 5), (6, 7)
WO_BANK, LN2_BANK, GATE_BANK = (0, 1, 4, 5, 3), (6, 7), 4
HU_BANK, HV_BANK = (2, 3), (0, 1)
F1_BANK, YU_BANK, YV_BANK, YP_BANK, F2_BANK = (5, 4), 6, 7, 0, (2, 3)
WARM_BANK, WARM_UP, WARM_START, WARM_NORM = 2, 13, 3, 14


def vit_tower(nc: bass.Bass, x, g1, wp, bp, g2, w_qkv, w_out, moe_w1, moe_b1, moe_w2, moe_b2,
              a1_w, a1_b, a2_w, a2_b, g_w, out):
    with ExitStack() as ctx:
        def sb(name, shape, dtype=F32):
            return ctx.enter_context(nc.sbuf_tensor(name, shape, dtype))

        def sem(name):
            return ctx.enter_context(nc.semaphore(name))

        def sems(*names):
            return [sem(name) for name in " ".join(names).split()]

        bank = [ctx.enter_context(nc.psum_tensor(f"bank{i}", [128, 512], F32)) for i in range(8)]

        wp_g = sb("wp_g", [128, KT, E])
        g1_sb = sb("g1_sb", [128, KT])
        bp_bc = sb("bp_bc", [P, E])
        g2_bc = sb("g2_bc", [P, E])
        b2_bc = sb("b2_bc", [P, E])
        wqk_hi, wqk_lo = (sb(name, [EH, 2, 8, HPAD], F32R) for name in ("wqk_hi", "wqk_lo"))
        wo = sb("wo", [EH, 2, E])
        w2 = sb("w2", [128, M, E])
        a1 = sb("a1", [EH + 1, NE, 2, F])
        a2 = sb("a2", [128, NE, M, E])
        b2u = sb("b2u", [T, E])
        b2v = sb("b2v", [T, E])
        gw = sb("gw", [EH, 2, NCLS, 2])
        ident = sb("ident", [128, 128])
        ones = sb("ones", [T, 1])
        neg_half = sb("neg_half", [P, NT])
        unparity = sb("unparity", [P, T])
        cls_mask = sb("cls_mask", [T, NCLS])
        slot_mask = sb("slot_mask", [QR, SLOTS])
        x_buf = sb("x_buf", [128, C * PATCH * IMG])
        x_sb = x_buf[0:B * G, :].rearrange("p (c f) -> p c f", c=C)
        xr_buf = sb("xr_buf", [128, C * G * PATCH * PATCH])
        x_r = xr_buf[0:B * G, :].rearrange("p (c w f) -> p c w f", c=C, w=G)
        xT_buf = sb("xT_buf", [128, KT * NTOK])
        xT = xT_buf[:].rearrange("p (k n) -> p k n", k=KT)
        squares = sb("squares", [T, PATCH, PATCH])
        h1 = xr_buf[:, 2 * B * SP:2 * B * SP + NT * E].rearrange("p (t e) -> p t e", t=NT)
        ss3 = sb("ss3", [T, C, G])
        ss = sb("ss", [T, G])
        ss_diag = sb("ss_diag", [T, N + 2, B])
        ms1 = sb("ms1", [P, NT])
        r1 = sb("r1", [P, NT])
        y = sb("y", [P, NT, E])
        y_sq = sb("y_sq", [P, E])
        ms2 = sb("ms2", [P, NT])
        ms2e = sb("ms2e", [P, NT])
        z = sb("z", [P, NT, E])
        r2 = sb("r2", [P, NT])
        h0 = sb("h0", [P, NT, E])
        stats = sb("stats", [P, 2, NT, 6])
        mv = sb("mv", [P, 2, NT, 2])
        eps_ms = sb("eps_ms", [P, NT])
        ve = sb("ve", [P, 2, NT])
        rs = sb("rs", [P, 2, NT])
        xn = sb("xn", [P, NT, E])
        nT_hi, nT_lo = (sb(name, [EH + 1, 2 * NTOK], F32R) for name in ("nT_hi", "nT_lo"))
        xnT_hi, xnT_lo = (h[0:EH, :].rearrange("r (k b n) -> r k b n", k=2, b=B) for h in (nT_hi, nT_lo))
        q_bd = xr_buf[0:QR, 0:2 * B * SP].rearrange("r (p b s n) -> r p b s n", p=2, b=B, s=SLOTS)
        k_bd = sb("k_bd", [QR, 2, B, 2, HPAD])
        s_max = sb("s_max", [SP, RING, 8])
        s_sub = sb("s_sub", [SP, RING, 8, N])
        e_sb = s_sub
        e_sum = sb("e_sum", [SP, RING, 8])
        e_inv = sb("e_inv", [SP, RING, 8])
        p_sb = sb("p_sb", [SP, RING, 8, HPAD])
        pT = sb("pT", [PR, 2, 4, SP])
        kp = sb("kp", [PR, 2, 4, SLOTS, 2, D])
        oT = sb("oT", [EH, 2, N, B])
        wqk = oT[:].rearrange("r p n b -> r (p n b)")[:, 0:2 * 8 * HPAD].rearrange("r (k g f) -> r k g f", k=2, g=8)
        h1b = y
        xn2 = z
        x2T = sb("x2T", [EH + 1, 2, T])
        x2_hi, x2_lo = (h[:, 0:2 * (NTOK - T)].rearrange("r (k n) -> r k n", k=2) for h in (nT_hi, nT_lo))
        w1 = x_buf[0:EH + 1, M * (NTOK - T):M * (NTOK - T) + 2 * F].rearrange("r (k f) -> r k f", k=2)
        w1_hi, w1_lo = (sb(name, [EH + 1, 2, F], F32R) for name in ("w1_hi", "w1_lo"))
        hT = x_buf[:, 0:M * (NTOK - T)].rearrange("p (m n) -> p m n", m=M)
        hu, hv = xT_buf[:, 0:F], xT_buf[:, F:2 * F]
        huT = xT_buf[:, 2 * F:2 * F + M * 2 * PPAD].rearrange("r (m v c) -> r m v c", m=M, v=2)
        hvT = xT_buf[:, 2 * F + M * 2 * PPAD:2 * F + M * (2 * PPAD + T)].rearrange("r (m c) -> r m c", m=M)
        yu_sb = y_sq
        x2P = sb("x2P", [EH + 1, 2, 2, PPAD])
        hc = sb("hc", [T, 2, E])
        lg6 = sb("lg6", [T, 2, NCLS])
        lg = sb("lg", [T, 2])
        gs = sb("gs", [T, 8])
        ge = sb("ge", [T, 2])
        gp = sb("gp", [T, 2])
        gk = sb("gk", [T, 2])
        gm = sb("gm", [T, 2])
        gn = sb("gn", [T, 2])
        cls_part = sb("cls_part", [T, E])
        res = xn

        x_in = [sem(f"x_in{c}") for c in range(C)]
        (x_top_in, wp_in, vec_in, wqk_in, wo_in, w1_in, a1_in, gw_in, w2_in, a2_in, out_done) = sems(
            "x_top_in wp_in vec_in wqk_in wo_in w1_in a1_in gw_in w2_in a2_in out_done")
        (consts, wpg_ready, wqk_low, r1_ready, z_ready, r2_ready, rs_ready, h0_ready, p_ready, w1_low,
         h1b_ready, pool_step) = sems(
            "consts wpg_ready wqk_low r1_ready z_ready r2_ready rs_ready h0_ready p_ready w1_low h1b_ready "
            "pool_step")
        (xt_ps, r1_ps, emb_ps, ln1_ps, qk_ps, s_ps, kp_ps, pt_ps, pv_ps, wo_ps, ln2_ps, gate_ps, hu_ps, hv_ps,
         huT_ps, hvT_ps, f1_ps, yu_ps, yv_ps, yp_ps, f2_ps) = sems(
            "xt_ps r1_ps emb_ps ln1_ps qk_ps s_ps kp_ps pt_ps pv_ps wo_ps ln2_ps gate_ps hu_ps hv_ps huT_ps "
            "hvT_ps f1_ps yu_ps yv_ps yp_ps f2_ps")
        (masks, xr_ready, xt_ready, diag_ready, ms1_ready, y_ready, zd_ready, eps_ready, stat_ready, mv_ready,
         ve_ready, xn_ready, xnl_ready, q_ready, kd_ready, max_ready, sub_ready, sum_ready, inv_ready, ov_ready,
         h1_ready, xn2_ready, x2l_ready, gate_step, hc_ready, eT_ready, yu_ready, part_ready, res_ready) = sems(
            "masks xr_ready xt_ready diag_ready ms1_ready y_ready zd_ready eps_ready stat_ready mv_ready "
            "ve_ready xn_ready xnl_ready q_ready kd_ready max_ready sub_ready sum_ready inv_ready ov_ready "
            "h1_ready xn2_ready x2l_ready gate_step hc_ready eT_ready yu_ready part_ready res_ready")
        (ss_ready, wqk_high, ms2_ready, xnh_ready, w1_high, k_ready, e_ready, pT_ready, kp_ready, oa_ready,
         x2T_ready, x2P_ready, x2h_ready, ge_ready, hu_ready, hv_ready, h_ready) = sems(
            "ss_ready wqk_high ms2_ready xnh_ready w1_high k_ready e_ready pT_ready kp_ready oa_ready "
            "x2T_ready x2P_ready x2h_ready ge_ready hu_ready hv_ready h_ready")

        block = ctx.enter_context(nc.Block())

        @block.sync
        def _(sp):
            x_rows = x.rearrange("b c (h p) w -> c b h (p w)", p=PATCH)
            w_rows = wp.rearrange("(q p c) e -> p q (c e)", q=2, c=C)
            half = PATCH * IMG // 2
            for q in range(2):
                rows = slice(q * half, (q + 1) * half)
                sp.dma_start(x_sb[:, 0, rows], x_rows[0][:, :, rows]).then_inc((x_top_in, x_in[0])[q], 16)
            sp.dma_start(wp_g[:].rearrange("p (q c) e -> p q (c e)", q=2), w_rows).then_inc(wp_in, 16)
            sp.dma_start(g1_sb[:].rearrange("p (q c) -> p q c", q=2),
                         g1.rearrange("(q p c) -> p q c", q=2, c=C)).then_inc(wp_in, 16)
            for c in range(1, C):
                sp.dma_start(x_sb[:, c, :], x_rows[c]).then_inc(x_in[c], 16)
            for vec, dst in ((bp, bp_bc), (g2, g2_bc), (moe_b2, b2_bc)):
                sp.dma_start(dst[:], vec.rearrange("(o e) -> o e", o=1).broadcast_to([P, E])).then_inc(vec_in, 16)
            for k in range(2):
                sp.dma_start(wqk[:, k, :, 0:HALF], w_qkv[k * EH:(k + 1) * EH, 0:2 * E]
                             .rearrange("r (g f) -> r g f", f=HALF)).then_inc(wqk_in, 16)
            sp.wait_ge(xr_ready, C + 1)
            sp.wait_ge(ss_ready, C * G + 1)
            sp.dma_start(w1[0:EH, :, :], moe_w1.rearrange("(k r) f -> r k f", k=2)).then_inc(w1_in, 16)
            sp.dma_start(w1[EH:EH + 1, 0, :], moe_b1.rearrange("(o f) -> o f", o=1)).then_inc(w1_in, 16)
            wo_rows = w_out.rearrange("(p g s d) e -> s p g d e", p=2, g=2, s=SLOTS)
            for s in range(SLOTS):
                for p in range(2):
                    sp.dma_start(wo[2 * D * s:2 * D * (s + 1), p, :], wo_rows[s, p]).then_inc(wo_in, 16)
            for k in range(2):
                sp.dma_start(gw[:, k, :, :], g_w[:, k * EH:(k + 1) * EH, :].rearrange("i r g -> r i g")) \
                    .then_inc(gw_in, 16)
            a1_rows = a1_w.rearrange("a (k r) f -> a r k f", k=2)
            for a in range(NE):
                sp.dma_start(a1[0:EH, a, :, :], a1_rows[a]).then_inc(a1_in, 16)
            sp.dma_start(a1[EH:EH + 1, :, 0, :], a1_b.rearrange("(o a) f -> o a f", o=1)).then_inc(a1_in, 16)
            for u in range(NU_E):
                rows = slice(2 * B * u, 2 * B * (u + 1))
                sp.dma_start(b2u[rows, :], a2_b[u:u + 1, :].broadcast_to([2 * B, E])).then_inc(a2_in, 16)
                for v in range(2):
                    rows = slice(B * (2 * u + v), B * (2 * u + v + 1))
                    sp.dma_start(b2v[rows, :], a2_b[3 + v:4 + v, :].broadcast_to([B, E])).then_inc(a2_in, 16)
            a2_rows = a2_w.rearrange("a (m r) e -> a r m e", m=M)
            for a in range(NE):
                sp.dma_start(a2[:, a, :, :], a2_rows[a]).then_inc(a2_in, 16)
            sp.dma_start(w2[:], moe_w2.rearrange("(m r) e -> r m e", m=M)).then_inc(w2_in, 16)
            out_rows = out.rearrange("b n e -> n b e")
            for t in range(NT):
                sp.wait_ge(res_ready, t + 1)
                sp.dma_start(out_rows[TN[t]:TN[t + 1]], res[0:ROWS[t], t, :]).then_inc(out_done, 16)
            sp.wait_ge(out_done, 16 * NT)

        @block.gpsimd
        def _(pool):
            nc.gpsimd.memset(ident[:], 0.0).then_inc(pool_step, 1)
            pool.wait_ge(pool_step, 1)
            nc.gpsimd.affine_select(out=ident[:], in_=ident[:], compare_op=ALU.not_equal, fill=1.0, base=0,
                                    pattern=[[-1, 128]], channel_multiplier=1).then_inc(consts, 1)
            pool.wait_ge(wp_in, 32)
            for kt in range(KT):
                k = (kt % 2) * C + kt // 2
                nc.gpsimd.tensor_tensor(wp_g[:, k, :], wp_g[:, k, :], g1_sb[:, k:k + 1].broadcast_to([128, E]),
                                        ALU.mult).then_inc(wpg_ready, 1)
            nc.gpsimd.memset(neg_half[:], -0.5).then_inc(consts, 1)
            nc.gpsimd.memset(ones[:], 1.0).then_inc(consts, 1)
            nc.gpsimd.memset(wqk[:, :, :, HALF:HPAD], 0.0).then_inc(consts, 1)
            nc.gpsimd.memset(p_sb[:], 0.0).then_inc(consts, 1)
            nc.gpsimd.memset(k_bd[:], 0.0).then_inc(consts, 1)
            pool.wait_ge(consts, 6)

            def split_wqk(k):
                nc.gpsimd.tensor_tensor(wqk_lo[:, k, :, :], wqk[:, k, :, :], wqk_hi[:, k, :, :],
                                        ALU.subtract).then_inc(wqk_low, 1)

            pool.wait_ge(wqk_high, 1)
            split_wqk(0)
            pool.wait_ge(ms1_ready, 1)
            nc.gpsimd.tensor_tensor(r1[:], ms1[:], neg_half[:], ALU.pow).then_inc(r1_ready, 1)
            split_wqk(1)

            def scaled(t):
                pool.wait_ge(y_ready, t + 1)
                nc.gpsimd.tensor_tensor(z[0:ROWS[t], t, :], y[0:ROWS[t], t, :], g2_bc[0:ROWS[t], :],
                                        ALU.mult).then_inc(z_ready, 1)

            def inverse_std(w, group, n):
                pool.wait_ge(ve_ready, n)
                cols = slice(*group)
                nc.gpsimd.tensor_tensor(rs[:, w, cols], ve[:, w, cols], neg_half[:, 0:group[1] - group[0]],
                                        ALU.pow).then_inc(rs_ready, 1)

            pool.wait_ge(vec_in, 48)
            scaled(1)
            scaled(2)
            scaled(3)
            inverse_std(0, GROUPS1[0], 1)
            inverse_std(0, GROUPS1[1], 2)
            inverse_std(0, GROUPS1[2], 3)
            pool.wait_ge(ms2_ready, NT)
            nc.gpsimd.tensor_scalar(ms2e[:], ms2[:], 1.0 / E, EPS_RMS, ALU.mult, ALU.add).then_inc(pool_step, 1)
            pool.wait_ge(pool_step, 2)
            nc.gpsimd.tensor_tensor(r2[:], ms2e[:], neg_half[:], ALU.pow).then_inc(r2_ready, 1)
            pool.wait_ge(r2_ready, 1)
            for t in range(NT):
                nc.gpsimd.tensor_tensor(h0[0:ROWS[t], t, :], z[0:ROWS[t], t, :],
                                        r2[0:ROWS[t], t:t + 1].broadcast_to([ROWS[t], E]),
                                        ALU.mult).then_inc(h0_ready, 1)
            pool.wait_ge(emb_ps, NT)
            nc.gpsimd.memset(huT, 0.0).then_inc(consts, 1)
            def low_w1(i):
                for k in range(2):
                    rows, cols = slice(0, EH + 1 - k), slice(i * F // W1_STEPS, (i + 1) * F // W1_STEPS)
                    nc.gpsimd.tensor_tensor(w1_lo[rows, k, cols], w1[rows, k, cols], w1_hi[rows, k, cols],
                                            ALU.subtract).then_inc(w1_low, 1)

            pool.wait_ge(w1_high, 2)
            for u in range(NU):
                pool.wait_ge(inv_ready, u + 1)
                if u >= RING:
                    pool.wait_ge(pt_ps, u - RING + 1)
                nc.gpsimd.tensor_tensor(p_sb[:, u % RING, :, 0:N], e_sb[:, u % RING, :, :],
                                        e_inv[:, u % RING, :].rearrange("p (k o) -> p k o", o=1)
                                        .broadcast_to([SP, 8, N]), ALU.mult).then_inc(p_ready, 1)
                if 1 <= u <= W1_STEPS:
                    low_w1(u - 1)
            for i, group in enumerate(GROUPS2):
                inverse_std(1, group, len(GROUPS1) + i + 1)
            pool.wait_ge(h1_ready, NT)
            for t in range(1, NT):
                nc.gpsimd.tensor_tensor(h1b[0:ROWS[t], t, :], h1[0:ROWS[t], t, :], b2_bc[0:ROWS[t], :],
                                        ALU.add).then_inc(h1b_ready, 1)

        @block.tensor
        def _(pe):
            pe.wait_ge(consts, 1)

            def keep_warm(n):
                for _ in range(n):
                    nc.tensor.transpose(bank[WARM_BANK][:, 0:128], ident[:], ident[:])

            keep_warm(WARM_UP)

            def transpose_patches(kt):
                c, q = kt // 2, kt % 2
                if c == 0 or q == 0:
                    pe.wait_ge(xr_ready, kt + 1 if c == 0 else c + 2)
                for half in range(2):
                    f = 2 * kt + half
                    if f >= 2:
                        pe.wait_ge(xt_ready, f - 1)
                    for w in range(3):
                        last = nc.tensor.transpose(bank[XT_BANK[f % 2]][:, w * T:(w + 1) * T],
                                                   x_r[:, c, 3 * half + w, q * 128:(q + 1) * 128], ident[0:T, 0:T])
                    last.then_inc(xt_ps, 1)

            def embed(kt, t):
                return nc.tensor.matmul(bank[EMB_BANK[t]][0:ROWS[t], 0:E], xT[:, kt, TN[t] * B:TN[t + 1] * B],
                                        wp_g[:, (kt % 2) * C + kt // 2, :], start=(kt == 0), stop=(kt == KT - 1))

            def embed_all(kt):
                pe.wait_ge(xt_ready, 2 * kt + 2)
                pe.wait_ge(wpg_ready, kt + 1)
                for t in range(NT):
                    embed(kt, t)

            transpose_patches(0)
            keep_warm(WARM_START)
            transpose_patches(1)
            for kt in range(KT - 3):
                embed_all(kt)
                transpose_patches(kt + 2)
            pe.wait_ge(wpg_ready, KT)
            embed(KT - 3, 0)
            embed(KT - 3, 1)
            pe.wait_ge(diag_ready, 2)
            pe.wait_ge(consts, 3)
            pe.wait_ge(masks, 11)
            for t in range(NT):
                last = nc.tensor.matmul(bank[R1_BANK][:, t:t + 1],
                                        ss_diag[:, TN[t]:TN[t] + P // B, :].rearrange("p n b -> p (n b)"),
                                        ones[:], start=True, stop=True)
            last.then_inc(r1_ps, 1)
            transpose_patches(KT - 1)
            embed(KT - 3, 2)
            embed(KT - 3, 3)
            pe.wait_ge(xt_ready, 2 * KT)
            for t in range(NT):
                if t == NT - 1:
                    embed(KT - 3, t)
                embed(KT - 2, t)
                embed(KT - 1, t).then_inc(emb_ps, 1)

            pe.wait_ge(ms1_ready, 1)
            keep_warm(WARM_NORM)
            for t in range(NT):
                pe.wait_ge(xn_ready, t + 1)
                for k in range(2):
                    last = nc.tensor.transpose(bank[LN1_BANK[t]][0:EH, k * ROWS[t]:(k + 1) * ROWS[t]],
                                               xn[0:ROWS[t], t, k * EH:(k + 1) * EH], ident[0:ROWS[t], 0:ROWS[t]])
                last.then_inc(ln1_ps, 1)

            def project(ch, outs):
                for s in outs:
                    o = 4 * ch + s
                    if o == 3:
                        pe.wait_ge(xnl_ready, 2 * NT)
                    if o >= len(QK_BANK):
                        pe.wait_ge(q_ready, o - len(QK_BANK) + 1)
                    n = 0
                    for k in range(2):
                        for w, x in ((wqk_hi, xnT_hi), (wqk_hi, xnT_lo), (wqk_lo, xnT_hi)):
                            last = nc.tensor.matmul(
                                bank[QK_BANK[o % len(QK_BANK)]][0:QR, 0:CHUNK * N],
                                w[:, k, 2 * s:2 * s + 2, :].rearrange("r g f -> r (g f)")[:, 0:QR],
                                x[:, k, ch * CHUNK:(ch + 1) * CHUNK, :].rearrange("r b n -> r (b n)"),
                                start=(n == 0), stop=(n == 5))
                            n += 1
                    last.then_inc(qk_ps, 1)

            pe.wait_ge(xnh_ready, NT)
            pe.wait_ge(xnl_ready, NT)
            pe.wait_ge(wqk_high, 1)
            pe.wait_ge(wqk_low, 2)
            pe.wait_ge(consts, 6)

            def scores(u):
                ch = u * UNIT // CHUNK
                pe.wait_ge(q_ready, 2 * (ch + 1))
                pe.wait_ge(k_ready, 3 * (ch + 1))
                pe.wait_ge(kd_ready, ch + 1)
                if u >= 2:
                    pe.wait_ge(sub_ready, u - 1)
                for i in range(UNIT):
                    for p in range(2):
                        n = 2 * i + p
                        last = nc.tensor.matmul(bank[S_BANK[u % 2]][0:SP, n * SC:(n + 1) * SC],
                                                q_bd[:, p, u * UNIT + i, :, :].rearrange("r s n -> r (s n)"),
                                                k_bd[:, p, u * UNIT + i, :, 0:N], start=True, stop=True)
                last.then_inc(s_ps, 1)

            def keys(u):
                pe.wait_ge(k_ready, 3 * (u * UNIT // CHUNK + 1))
                pe.wait_ge(kd_ready, u * UNIT // CHUNK + 1)
                if u >= 2:
                    pe.wait_ge(kp_ready, 2 * (u - 1))
                for i in range(UNIT):
                    for p in range(2):
                        n = 2 * i + p
                        last = nc.tensor.transpose(
                            bank[KP_BANK[u % 2]][0:PR, n * QR:(n + 1) * QR],
                            k_bd[:, p, u * UNIT + i, :, :].rearrange("r g j -> r (g j)")[:, 0:PR], ident[0:QR, 0:QR])
                last.then_inc(kp_ps, 1)

            def probs(u):
                pe.wait_ge(p_ready, u + 1)
                if u < 2:
                    pe.wait_ge(q_ready, 3 + u)
                if u >= 2:
                    pe.wait_ge(pT_ready, u - 1)
                for n in range(2 * UNIT):
                    last = nc.tensor.transpose(
                        bank[PT_BANK[u % 2]][0:PR, n * SP:(n + 1) * SP],
                        p_sb[:, u % RING, 2 * n:2 * n + 2, :].rearrange("r g j -> r (g j)")[:, 0:PR], ident[0:SP, 0:SP])
                last.then_inc(pt_ps, 1)

            def values(u):
                pe.wait_ge(pT_ready, u + 1)
                pe.wait_ge(kp_ready, 2 * (u + 1))
                if u == 0:
                    pe.wait_ge(k_ready, 6)
                    pe.wait_ge(kd_ready, 2)
                if u >= 2:
                    pe.wait_ge(ov_ready, u - 1)
                    pe.wait_ge(oa_ready, 2 * (u - 1))
                for n in range(2 * UNIT):
                    last = nc.tensor.matmul(bank[PV_BANK[u % 2]][0:EH, n * SP:(n + 1) * SP],
                                            kp[:, u % 2, n].rearrange("r s g d -> r (s g d)"),
                                            pT[:, u % 2, n, :], start=True, stop=True)
                last.then_inc(pv_ps, 1)

            project(0, range(4))
            project(1, range(1))
            scores(0)
            scores(1)
            keys(0)
            project(1, range(1, 4))
            scores(2)
            probs(0)
            for u in range(NU):
                if u + 1 < NU:
                    probs(u + 1)
                if u + RING < NU:
                    scores(u + RING)
                if u + 1 < NU:
                    keys(u + 1)
                values(u)

            pe.wait_ge(ov_ready, NU)
            pe.wait_ge(oa_ready, 2 * NU)
            pe.wait_ge(wo_in, 96)
            for t in range(NT):
                for p in range(2):
                    last = nc.tensor.matmul(bank[WO_BANK[t]][0:ROWS[t], 0:E],
                                            oT[:, p, TN[t]:TN[t + 1], :].rearrange("r n b -> r (n b)"),
                                            wo[:, p, :], start=(p == 0), stop=(p == 1))
                last.then_inc(wo_ps, 1)

            def transpose_ln2(t):
                pe.wait_ge(xn2_ready, t + 1)
                if t == 2:
                    pe.wait_ge(x2P_ready, 2)
                if t >= 3:
                    pe.wait_ge(x2l_ready, t - 2)
                for k in range(2):
                    last = nc.tensor.transpose(bank[LN2_BANK[t % 2]][0:EH, k * ROWS[t]:(k + 1) * ROWS[t]],
                                               xn2[0:ROWS[t], t, k * EH:(k + 1) * EH], ident[0:ROWS[t], 0:ROWS[t]])
                last.then_inc(ln2_ps, 1)

            def hidden_u(j):
                cols = slice(*HALVES[j])
                for k in range(2):
                    rows = EH + 1 - k
                    for u in range(NU_E):
                        tok = slice(2 * B * u, 2 * B * (u + 1))
                        last = nc.tensor.matmul(bank[HU_BANK[j]][tok, 0:cols.stop - cols.start], x2T[0:rows, k, tok],
                                                a1[0:rows, u, k, cols], start=(k == 0), stop=(k == 1))
                last.then_inc(hu_ps, 1)

            def hidden_v(j):
                cols = slice(*HALVES[j])
                for k in range(2):
                    rows = EH + 1 - k
                    for v in range(2):
                        last = nc.tensor.matmul(
                            bank[HV_BANK[j]][PPAD * v:PPAD * (v + 1), 0:cols.stop - cols.start],
                            x2P[0:rows, k, v, :], a1[0:rows, 3 + v, k, cols], start=(k == 0), stop=(k == 1))
                last.then_inc(hv_ps, 1)

            def transpose_hidden(src, rows, banks, done):
                for j in range(2):
                    for i in range(3):
                        m = 3 * j + i
                        last = nc.tensor.transpose(bank[banks[j]][:, i * rows:(i + 1) * rows],
                                                   src[0:rows, m * 128:(m + 1) * 128], ident[0:rows, 0:rows])
                    last.then_inc(done, 1)

            def patch_hidden(m):
                if m >= 2:
                    pe.wait_ge(h_ready, m - 1)
                cols = slice(m * 128, (m + 1) * 128)
                n = 0
                for k in range(2):
                    rows = EH + 1 - k
                    for w, x2 in ((w1_hi, x2_hi), (w1_hi, x2_lo), (w1_lo, x2_hi)):
                        last = nc.tensor.matmul(bank[F1_BANK[m % 2]][:, 0:NTOK - T], w[0:rows, k, cols],
                                                x2[0:rows, k, :], start=(n == 0), stop=(n == 5))
                        n += 1
                last.then_inc(f1_ps, 1)

            transpose_ln2(0)
            pe.wait_ge(x2T_ready, 1)
            pe.wait_ge(gw_in, 32)
            pe.wait_ge(masks, 11)
            pe.wait_ge(h1_ready, 3)
            for k in range(2):
                last = nc.tensor.matmul(bank[GATE_BANK][0:T, 0:2 * NCLS], x2T[0:EH, k, 0:T],
                                        gw[:, k, :, :].rearrange("r i g -> r (i g)"), start=(k == 0), stop=(k == 1))
            last.then_inc(gate_ps, 1)
            pe.wait_ge(a1_in, 16 * (NE + 1))
            hidden_u(0)
            transpose_ln2(1)
            transpose_ln2(2)
            pe.wait_ge(h1_ready, NT)
            hidden_u(1)
            transpose_ln2(3)
            transpose_ln2(4)
            hidden_v(0)
            hidden_v(1)
            pe.wait_ge(x2h_ready, NT - 1)
            pe.wait_ge(x2l_ready, NT - 1)
            pe.wait_ge(w1_low, 2 * W1_STEPS)
            patch_hidden(0)
            pe.wait_ge(gate_step, 1)
            patch_hidden(1)
            pe.wait_ge(hu_ready, 2)
            transpose_hidden(hu, T, HU_BANK, huT_ps)
            patch_hidden(2)
            pe.wait_ge(hv_ready, 2)
            transpose_hidden(hv, 2 * PPAD, HV_BANK, hvT_ps)
            for m in range(3, M):
                patch_hidden(m)
            pe.wait_ge(eT_ready, 8)
            pe.wait_ge(a2_in, 16 * (3 * NU_E + NE))
            for m in range(M):
                for v in range(2):
                    last = nc.tensor.matmul(bank[YU_BANK][PPAD * v:PPAD * (v + 1), 0:E], huT[:, m, v, :],
                                            a2[:, 3 + v, m, :], start=(m == 0), stop=(m == M - 1))
            last.then_inc(yu_ps, 1)
            for m in range(M):
                for u in range(NU_E):
                    tok = slice(2 * B * u, 2 * B * (u + 1))
                    last = nc.tensor.matmul(bank[YV_BANK][tok, 0:E], hvT[:, m, tok], a2[:, u, m, :],
                                            start=(m == 0), stop=(m == M - 1))
            last.then_inc(yv_ps, 1)
            pe.wait_ge(yu_ready, 1)
            nc.tensor.matmul(bank[YP_BANK][0:T, 0:E], unparity[:], yu_sb[:], start=True, stop=True).then_inc(yp_ps, 1)
            pe.wait_ge(h_ready, M)
            pe.wait_ge(w2_in, 16)
            for t in range(1, NT):
                if t >= 3:
                    pe.wait_ge(res_ready, t - 1)
                for m in range(M):
                    last = nc.tensor.matmul(bank[F2_BANK[t % 2]][0:ROWS[t], 0:E],
                                            hT[:, m, TN[t] * B - T:TN[t + 1] * B - T], w2[:, m, :],
                                            start=(m == 0), stop=(m == M - 1))
                last.then_inc(f2_ps, 1)

        @block.scalar
        def _(act):
            act.wait_ge(consts, 1)
            nc.scalar.activation(squares[:, 0, :], ident[0:T, 0:PATCH], ACT.Square).then_inc(ss_ready, 1)
            patches = x_sb.rearrange("p c (r w f) -> p c w r f", r=PATCH, w=G)
            for c in range(C):
                if c == 0:
                    act.wait_ge(x_top_in, 16)
                act.wait_ge(x_in[c], 16)
                for w in range(G):
                    act.wait_ge(ss_ready, c * G + w + 1)
                    nc.scalar.activation(squares[:], patches[:, c, w], ACT.Square,
                                         accum_out=ss3[:, c, w:w + 1]).then_inc(ss_ready, 1)
            act.wait_ge(wqk_in, 32)
            act.wait_ge(consts, 4)
            nc.scalar.activation(wqk_hi[:], wqk, ACT.Copy).then_inc(wqk_high, 1)
            act.wait_ge(masks, 11)
            for t in range(NT):
                act.wait_ge(y_ready, t + 1)
                if t >= 1:
                    act.wait_ge(ms2_ready, t)
                nc.scalar.activation(y_sq[0:ROWS[t], :], y[0:ROWS[t], t, :], ACT.Square,
                                     accum_out=ms2[0:ROWS[t], t:t + 1]).then_inc(ms2_ready, 1)
            for t in range(NT):
                act.wait_ge(ln1_ps, t + 1)
                src, hi, _ = token_block(bank, xnT_hi, xnT_lo, t, slice(0, B))
                nc.scalar.activation(hi, src, ACT.Copy).then_inc(xnh_ready, 1)
            act.wait_ge(w1_in, 32)
            for k in range(2):
                nc.scalar.activation(w1_hi[0:EH + 1 - k, k, :], w1[0:EH + 1 - k, k, :], ACT.Copy).then_inc(w1_high, 1)


            def take_k(ch):
                for p, hg in ((0, 0), (0, 1), (1, 0)):
                    act.wait_ge(qk_ps, 4 * ch + 2 + p + 1)
                    nc.scalar.activation(*key_block(k_bd, bank, ch, p, hg), ACT.Copy).then_inc(k_ready, 1)

            def exponentials(u):
                act.wait_ge(sub_ready, u + 1)
                nc.scalar.activation(e_sb[:, u % RING, :, :], s_sub[:, u % RING, :, :], ACT.Exp,
                                     scale=float(E) ** -0.5).then_inc(e_ready, 1)

            def copy_keys(u):
                act.wait_ge(kp_ps, u + 1)
                if u >= 2:
                    act.wait_ge(pv_ps, u - 1)
                src = bank[KP_BANK[u % 2]][0:PR, 0:4 * QR].rearrange("r (n c) -> r n c", n=4)
                for hg in range(2):
                    nc.scalar.activation(kp[:, u % 2, :, :, hg, :], src[:, :, hg * HPAD:hg * HPAD + HALF]
                                         .rearrange("r n (s d) -> r n s d", s=SLOTS), ACT.Copy).then_inc(kp_ready, 1)

            def copy_probs(u):
                act.wait_ge(pt_ps, u + 1)
                if u >= 2:
                    act.wait_ge(pv_ps, u - 1)
                nc.scalar.activation(pT[:, u % 2, :, :], bank[PT_BANK[u % 2]][0:PR, 0:4 * SP]
                                     .rearrange("r (n c) -> r n c", n=4), ACT.Copy).then_inc(pT_ready, 1)

            def take_values(u):
                act.wait_ge(pv_ps, u + 1)
                for s in (0, 1):
                    nc.scalar.activation(*value_block(oT, bank, u, s), ACT.Copy).then_inc(oa_ready, 1)

            act.wait_ge(consts, 6)
            take_k(0)
            exponentials(0)
            copy_keys(0)
            exponentials(1)
            take_k(1)
            exponentials(2)
            copy_probs(0)
            for u in range(NU):
                if u + 1 < NU:
                    copy_probs(u + 1)
                if u + 1 < NU:
                    copy_keys(u + 1)
                if u + RING < NU:
                    exponentials(u + RING)
                take_values(u)

            act.wait_ge(ln2_ps, 1)
            nc.scalar.activation(x2T[0:EH, :, :], bank[LN2_BANK[0]][0:EH, 0:2 * T].rearrange("r (k c) -> r k c", k=2),
                                 ACT.Copy).then_inc(x2T_ready, 1)
            for k in range(2):
                nc.scalar.activation(x2P[0:EH, k, :, 0:PPAD - B].rearrange("r v (u b) -> r v u b", u=NU_E),
                                     bank[LN2_BANK[0]][0:EH, k * T:(k + 1) * T]
                                     .rearrange("r (u v b) -> r v u b", u=NU_E, v=2), ACT.Copy).then_inc(x2P_ready, 1)
            act.wait_ge(masks, 11)
            for t in range(1, NT):
                act.wait_ge(ln2_ps, t + 1)
                nc.scalar.activation(x2_hi[0:EH, :, TN[t] * B - T:TN[t + 1] * B - T],
                                     bank[LN2_BANK[t % 2]][0:EH, 0:2 * ROWS[t]].rearrange("r (k c) -> r k c", k=2),
                                     ACT.Copy).then_inc(x2h_ready, 1)
            act.wait_ge(gate_step, 4)
            nc.scalar.activation(ge[:], gs[:, 1:3], ACT.Exp).then_inc(ge_ready, 1)
            for dst, rows, banks, done, ready in ((hu, T, HU_BANK, hu_ps, hu_ready),
                                                  (hv, 2 * PPAD, HV_BANK, hv_ps, hv_ready)):
                for j, (a, b) in enumerate(HALVES):
                    act.wait_ge(done, j + 1)
                    nc.scalar.activation(dst[0:rows, a:b], bank[banks[j]][0:rows, 0:b - a], ACT.Gelu) \
                        .then_inc(ready, 1)
            for m in range(M):
                act.wait_ge(f1_ps, m + 1)
                nc.scalar.activation(hT[:, m, :], bank[F1_BANK[m % 2]][:, 0:NTOK - T], ACT.Gelu).then_inc(h_ready, 1)

        @block.vector
        def _(dve):
            dve.wait_ge(consts, 1)
            nc.vector.tensor_reduce(cls_mask[:], ident[0:T, 0:T].rearrange("p (i b) -> p i b", i=NCLS), AX.X,
                                    ALU.add).then_inc(masks, 1)
            nc.vector.tensor_reduce(
                slot_mask[:], ident[0:QR, :].rearrange("p (g f) -> p g f", g=2)[:, :, 0:HALF]
                .rearrange("p g (s d) -> p s g d", s=SLOTS), AX.XY, ALU.add).then_inc(masks, 1)
            nc.vector.memset(x2T[EH:EH + 1, 0, :], 1.0).then_inc(masks, 1)
            nc.vector.tensor_copy(x2_hi[EH:EH + 1, 0, :], ident[0:1, 0:1].broadcast_to([1, NTOK - T])).then_inc(masks, 1)
            nc.vector.tensor_copy(x2_lo[EH:EH + 1, 0, :], ident[0:1, 1:2].broadcast_to([1, NTOK - T])).then_inc(masks, 1)
            nc.vector.memset(x2P[EH:EH + 1, 0, :, :], 1.0).then_inc(masks, 1)
            nc.vector.memset(x2P[0:EH, :, :, PPAD - B:PPAD], 0.0).then_inc(masks, 1)

            nc.vector.memset(ms2[:], 0.0).then_inc(masks, 1)
            nc.vector.memset(mv[:], 0.0).then_inc(masks, 1)
            nc.vector.memset(ss_diag[:, N:N + 2, :], 0.0).then_inc(masks, 1)
            nc.vector.tensor_copy(unparity[:].rearrange("p (u v b) -> p v u b", u=NU_E, v=2),
                                  ident[:].rearrange("p (v c) -> p v c", v=2)[:, :, 0:PPAD - B]
                                  .rearrange("p v (u b) -> p v u b", u=NU_E)).then_inc(masks, 1)

            def regroup_half(q):
                dve.wait_ge((x_top_in, x_in[0])[q], 16)
                nc.vector.tensor_copy(
                    x_r[:, 0, :, q * 128:(q + 1) * 128].rearrange("p w (r f) -> p w r f", f=PATCH),
                    x_sb[:, 0, q * PATCH * IMG // 2:(q + 1) * PATCH * IMG // 2]
                    .rearrange("p (r w f) -> p w r f", w=G, f=PATCH)).then_inc(xr_ready, 1)

            def regroup(c):
                dve.wait_ge(x_in[c], 16)
                nc.vector.tensor_copy(x_r[:, c, :, :].rearrange("p w (r f) -> p w r f", r=PATCH),
                                      x_sb[:, c, :].rearrange("p (r w f) -> p w r f", r=PATCH, w=G)) \
                    .then_inc(xr_ready, 1)

            def spread_sums():
                dve.wait_ge(ss_ready, C * G + 1)
                nc.vector.tensor_reduce(ss[:], ss3[:].rearrange("p c w -> p w c"), AX.X,
                                        ALU.add).then_inc(diag_ready, 1)
                dve.wait_ge(diag_ready, 1)
                nc.vector.tensor_tensor(ss_diag[:, 0:N, :].rearrange("p (h w) b -> p h w b", h=G),
                                        ss[:].rearrange("p (h w b) -> p h w b", h=1, b=1).broadcast_to([T, G, G, B]),
                                        ident[0:T, 0:T].rearrange("p (b h w) -> p h w b", b=B, w=1)
                                        .broadcast_to([T, G, G, B]), ALU.mult).then_inc(diag_ready, 1)

            def mean_squares():
                dve.wait_ge(r1_ps, 1)
                nc.vector.tensor_scalar(ms1[:], bank[R1_BANK][:, 0:NT], 1.0 / PD, EPS_RMS, ALU.mult,
                                        ALU.add).then_inc(ms1_ready, 1)

            regroup_half(0)
            regroup_half(1)
            for f in range(2 * KT):
                if f in (4, 6):
                    regroup(f // 2 - 1)
                if f == 8:
                    spread_sums()
                if f == 10:
                    mean_squares()
                kt, half = f // 2, f % 2
                dve.wait_ge(xt_ps, f + 1)
                nc.vector.tensor_copy(
                    xT[:, kt, :].rearrange("r (h w b) -> r w b h", h=G, w=G)[:, 3 * half:3 * half + 3],
                    bank[XT_BANK[f % 2]][:, 0:3 * T].rearrange("r (w b h) -> r w b h", w=3, b=B)).then_inc(xt_ready, 1)

            dve.wait_ge(vec_in, 48)
            dve.wait_ge(masks, 11)

            def embedded(t):
                dve.wait_ge(emb_ps, t + 1)
                if t == 0:
                    dve.wait_ge(r1_ready, 1)
                nc.vector.scalar_tensor_tensor(out=y[0:ROWS[t], t, :], in0=bank[EMB_BANK[t]][0:ROWS[t], 0:E],
                                               scalar=r1[0:ROWS[t], t:t + 1], in1=bp_bc[0:ROWS[t], :], op0=ALU.mult,
                                               op1=ALU.add).then_inc(y_ready, 1)

            def scaled(t):
                dve.wait_ge(y_ready, t + 1)
                nc.vector.tensor_tensor(z[0:ROWS[t], t, :], y[0:ROWS[t], t, :], g2_bc[0:ROWS[t], :],
                                        ALU.mult).then_inc(zd_ready, 1)

            def statistics(w, h, t, ready, n):
                dve.wait_ge(ready, n)
                nc.vector.bn_stats(stats[0:ROWS[t], w, t, :], h[0:ROWS[t], t, :]).then_inc(stat_ready, 1)

            def moments(w, t):
                dve.wait_ge(stat_ready, NT * w + t + 1)
                nc.vector.bn_aggr(mv[0:ROWS[t], w, t, :], stats[0:ROWS[t], w, t, :]).then_inc(mv_ready, 1)

            def variance1(g):
                cols = slice(*GROUPS1[g])
                dve.wait_ge(eps_ready, g + 1)
                dve.wait_ge(mv_ready, GROUPS1[g][1])
                nc.vector.tensor_tensor(ve[:, 0, cols], eps_ms[:, cols], mv[:, 0, cols, 1], ALU.add).then_inc(ve_ready, 1)

            def eps1(g):
                cols = slice(*GROUPS1[g])
                dve.wait_ge(ms2_ready, GROUPS1[g][1])
                nc.vector.tensor_scalar(eps_ms[:, cols], ms2[:, cols], EPS_LN / E, EPS_LN * EPS_RMS, ALU.mult,
                                        ALU.add).then_inc(eps_ready, 1)

            def variance2(g):
                cols = slice(*GROUPS2[g])
                dve.wait_ge(mv_ready, NT + GROUPS2[g][1])
                nc.vector.tensor_scalar(ve[:, 1, cols], mv[:, 1, cols, 1], EPS_LN, None, ALU.add).then_inc(ve_ready, 1)

            def normalise(w, h, dst, g, ready, tiles):
                dve.wait_ge(rs_ready, len(GROUPS1) * w + g + 1)
                for t in tiles:
                    nc.vector.tensor_scalar(dst[0:ROWS[t], t, :], h[0:ROWS[t], t, :], mv[0:ROWS[t], w, t, 0:1],
                                            rs[0:ROWS[t], w, t:t + 1], ALU.subtract, ALU.mult).then_inc(ready, 1)

            embedded(0)
            scaled(0)
            embedded(1)
            statistics(0, z, 0, zd_ready, 1)
            embedded(2)
            embedded(3)
            statistics(0, z, 1, z_ready, 1)
            eps1(0)
            moments(0, 0)
            moments(0, 1)
            embedded(4)
            variance1(0)
            statistics(0, z, 2, z_ready, 2)
            statistics(0, z, 3, z_ready, 3)
            scaled(4)
            eps1(1)
            moments(0, 2)
            moments(0, 3)
            statistics(0, z, 4, zd_ready, 2)
            variance1(1)
            eps1(2)
            moments(0, 4)
            normalise(0, z, xn, 0, xn_ready, (0,))
            variance1(2)
            normalise(0, z, xn, 0, xn_ready, (1,))
            normalise(0, z, xn, 1, xn_ready, (2, 3))
            normalise(0, z, xn, 2, xn_ready, (4,))

            for ch in range(B // CHUNK):
                for t in range(NT):
                    dve.wait_ge(xnh_ready, t + 1)
                    src, hi, lo = token_block(bank, xnT_hi, xnT_lo, t, slice(ch * CHUNK, (ch + 1) * CHUNK))
                    nc.vector.tensor_tensor(lo, src, hi, ALU.subtract).then_inc(xnl_ready, 1)

            def take_q(o, p, ch):
                dve.wait_ge(qk_ps, o + 1)
                nc.vector.tensor_tensor(
                    q_bd[:, p, ch * CHUNK:(ch + 1) * CHUNK, :, :],
                    bank[QK_BANK[o % len(QK_BANK)]][0:QR, 0:CHUNK * N].rearrange("r (b o n) -> r b o n", b=CHUNK, o=1)
                    .broadcast_to([QR, CHUNK, SLOTS, N]),
                    slot_mask[:].rearrange("r (o s q) -> r o s q", o=1, q=1)
                    .broadcast_to([QR, CHUNK, SLOTS, N]), ALU.mult).then_inc(q_ready, 1)

            def row_max(u):
                dve.wait_ge(s_ps, u + 1)
                s = bank[S_BANK[u % 2]][0:SP, 0:8 * N].rearrange("p (k j) -> p k j", k=8)
                if u >= RING:
                    dve.wait_ge(sub_ready, u - RING + 1)
                nc.vector.tensor_reduce(s_max[:, u % RING, :], s, AX.X, ALU.max).then_inc(max_ready, 1)

            def subtract_max(u):
                dve.wait_ge(max_ready, u + 1)
                if u >= RING:
                    dve.wait_ge(p_ready, u - RING + 1)
                    dve.wait_ge(sum_ready, u - RING + 1)
                s = bank[S_BANK[u % 2]][0:SP, 0:8 * N].rearrange("p (k j) -> p k j", k=8)
                nc.vector.tensor_tensor(s_sub[:, u % RING, :, :], s, s_max[:, u % RING, :]
                                        .rearrange("p (k o) -> p k o", o=1).broadcast_to([SP, 8, N]),
                                        ALU.subtract).then_inc(sub_ready, 1)

            def row_sum(u):
                dve.wait_ge(e_ready, u + 1)
                if u >= RING:
                    dve.wait_ge(inv_ready, u - RING + 1)
                nc.vector.tensor_reduce(e_sum[:, u % RING, :], e_sb[:, u % RING, :, :], AX.X,
                                        ALU.add).then_inc(sum_ready, 1)

            def invert_sum(u):
                dve.wait_ge(sum_ready, u + 1)
                if u >= RING:
                    dve.wait_ge(p_ready, u - RING + 1)
                nc.vector.reciprocal(e_inv[:, u % RING, :], e_sum[:, u % RING, :]).then_inc(inv_ready, 1)

            def take_values(u):
                dve.wait_ge(pv_ps, u + 1)
                nc.vector.tensor_copy(*value_block(oT, bank, u, 2)).then_inc(ov_ready, 1)

            def shift(u):
                row_max(u)
                subtract_max(u)

            def sums(u):
                row_sum(u)
                invert_sum(u)

            def take_k(ch):
                dve.wait_ge(qk_ps, 4 * ch + 4)
                if ch == 0:
                    dve.wait_ge(consts, 6)
                nc.vector.tensor_copy(*key_block(k_bd, bank, ch, 1, 1)).then_inc(kd_ready, 1)

            take_q(0, 0, 0)
            take_q(1, 1, 0)
            take_k(0)
            take_q(4, 0, 1)
            shift(0)
            shift(1)
            sums(0)
            sums(1)
            take_q(5, 1, 1)
            shift(2)
            take_k(1)
            for u in range(NU):
                if u + 2 < NU:
                    sums(u + 2)
                if u + RING < NU:
                    shift(u + RING)
                take_values(u)

            def split_tokens(t):
                cols = slice(TN[t] * B - T, TN[t + 1] * B - T)
                src = bank[LN2_BANK[t % 2]][0:EH, 0:2 * ROWS[t]].rearrange("r (k c) -> r k c", k=2)
                dve.wait_ge(ln2_ps, t + 1)
                dve.wait_ge(x2h_ready, t)
                nc.vector.tensor_tensor(x2_lo[0:EH, :, cols], src, x2_hi[0:EH, :, cols],
                                        ALU.subtract).then_inc(x2l_ready, 1)

            dve.wait_ge(h0_ready, NT)

            def residual(t):
                dve.wait_ge(wo_ps, t + 1)
                nc.vector.tensor_tensor(h1[0:ROWS[t], t, :], bank[WO_BANK[t]][0:ROWS[t], 0:E], h0[0:ROWS[t], t, :],
                                        ALU.add).then_inc(h1_ready, 1)

            residual(0)
            statistics(1, h1, 0, h1_ready, 1)
            moments(1, 0)
            variance2(0)
            residual(1)
            statistics(1, h1, 1, h1_ready, 2)
            residual(2)
            normalise(1, h1, xn2, 0, xn2_ready, range(*GROUPS2[0]))
            statistics(1, h1, 2, h1_ready, 3)
            moments(1, 1)
            moments(1, 2)
            variance2(1)
            residual(3)
            statistics(1, h1, 3, h1_ready, 4)
            residual(4)
            normalise(1, h1, xn2, 1, xn2_ready, range(*GROUPS2[1]))
            statistics(1, h1, 4, h1_ready, 5)
            moments(1, 3)
            moments(1, 4)
            variance2(2)
            split_tokens(1)
            normalise(1, h1, xn2, 2, xn2_ready, range(*GROUPS2[2]))
            split_tokens(2)

            dve.wait_ge(gate_ps, 1)
            nc.vector.tensor_tensor(lg6[:], bank[GATE_BANK][0:T, 0:2 * NCLS].rearrange("p (i g) -> p g i", g=2),
                                    cls_mask[:].rearrange("p (o i) -> p o i", o=1).broadcast_to([T, 2, NCLS]),
                                    ALU.mult).then_inc(gate_step, 1)
            dve.wait_ge(gate_step, 1)
            nc.vector.tensor_reduce(lg[:], lg6[:], AX.X, ALU.add).then_inc(gate_step, 1)
            dve.wait_ge(gate_step, 2)
            nc.vector.tensor_reduce(gs[:, 0:1], lg[:], AX.X, ALU.max).then_inc(gate_step, 1)
            dve.wait_ge(gate_step, 3)
            nc.vector.tensor_scalar(gs[:, 1:3], lg[:], gs[:, 0:1], None, ALU.subtract).then_inc(gate_step, 1)
            split_tokens(3)
            split_tokens(4)
            dve.wait_ge(ge_ready, 1)
            nc.vector.tensor_reduce(gs[:, 3:4], ge[:], AX.X, ALU.add).then_inc(gate_step, 1)
            dve.wait_ge(gate_step, 5)
            nc.vector.reciprocal(gs[:, 4:5], gs[:, 3:4]).then_inc(gate_step, 1)
            dve.wait_ge(gate_step, 6)
            nc.vector.tensor_scalar(gp[:], ge[:], gs[:, 4:5], None, ALU.mult).then_inc(gate_step, 1)
            dve.wait_ge(gate_step, 7)
            nc.vector.tensor_reduce(gs[:, 5:6], gp[:], AX.X, ALU.min).then_inc(gate_step, 1)
            dve.wait_ge(gate_step, 8)
            nc.vector.tensor_scalar(gk[:], gp[:], gs[:, 5:6], None, ALU.is_gt).then_inc(gate_step, 1)
            dve.wait_ge(gate_step, 9)
            nc.vector.tensor_tensor(gm[:], gp[:], gk[:], ALU.mult).then_inc(gate_step, 1)
            dve.wait_ge(gate_step, 10)
            nc.vector.tensor_reduce(gs[:, 6:7], gm[:], AX.X, ALU.add).then_inc(gate_step, 1)
            dve.wait_ge(gate_step, 11)
            nc.vector.tensor_scalar(gs[:, 7:8], gs[:, 6:7], 1e-6, None, ALU.max).then_inc(gate_step, 1)
            dve.wait_ge(gate_step, 12)
            nc.vector.reciprocal(gs[:, 3:4], gs[:, 7:8]).then_inc(gate_step, 1)
            dve.wait_ge(gate_step, 13)
            nc.vector.tensor_scalar(gn[:], gm[:], gs[:, 3:4], None, ALU.mult).then_inc(gate_step, 1)
            dve.wait_ge(gate_step, 14)
            dve.wait_ge(a2_in, 16 * (3 * NU_E + NE))
            nc.vector.scalar_tensor_tensor(out=hc[:, 0, :], in0=b2v[:], scalar=gn[:, 0:1], in1=h1[0:T, 0, :],
                                           op0=ALU.mult, op1=ALU.add).then_inc(hc_ready, 1)
            dve.wait_ge(hc_ready, 1)
            nc.vector.scalar_tensor_tensor(out=hc[:, 1, :], in0=b2u[:], scalar=gn[:, 1:2], in1=hc[:, 0, :],
                                           op0=ALU.mult, op1=ALU.add).then_inc(hc_ready, 1)
            dve.wait_ge(consts, 7)
            for j in range(2):
                dve.wait_ge(huT_ps, j + 1)
                for v in range(2):
                    nc.vector.tensor_copy(
                        huT[:, 3 * j:3 * j + 3, v, 0:PPAD - B].rearrange("r m (u b) -> r m u b", u=NU_E),
                        bank[HU_BANK[j]][:, 0:3 * T].rearrange("r (m u v b) -> r m u v b", m=3, u=NU_E, v=2)
                        [:, :, :, v, :]).then_inc(eT_ready, 1)
            for j in range(2):
                dve.wait_ge(hvT_ps, j + 1)
                for v in range(2):
                    nc.vector.tensor_copy(
                        hvT[:, 3 * j:3 * j + 3, :].rearrange("r m (u v b) -> r m u v b", u=NU_E, v=2)[:, :, :, v, :],
                        bank[HV_BANK[j]][:, 0:6 * PPAD].rearrange("r (m v c) -> r m v c", m=3, v=2)
                        [:, :, v, 0:PPAD - B].rearrange("r m (u b) -> r m u b", u=NU_E)).then_inc(eT_ready, 1)
            dve.wait_ge(yu_ps, 1)
            nc.vector.tensor_copy(yu_sb[:], bank[YU_BANK][:, 0:E]).then_inc(yu_ready, 1)
            dve.wait_ge(yp_ps, 1)
            dve.wait_ge(hc_ready, 2)
            nc.vector.scalar_tensor_tensor(out=cls_part[:], in0=bank[YP_BANK][0:T, 0:E], scalar=gn[:, 0:1],
                                           in1=hc[:, 1, :], op0=ALU.mult, op1=ALU.add).then_inc(part_ready, 1)
            dve.wait_ge(yv_ps, 1)
            dve.wait_ge(part_ready, 1)
            nc.vector.scalar_tensor_tensor(out=res[0:T, 0, :], in0=bank[YV_BANK][0:T, 0:E], scalar=gn[:, 1:2],
                                           in1=cls_part[:], op0=ALU.mult, op1=ALU.add).then_inc(res_ready, 1)
            for t in range(1, NT):
                dve.wait_ge(h1b_ready, t)
                dve.wait_ge(f2_ps, t)
                nc.vector.tensor_tensor(res[0:ROWS[t], t, :], bank[F2_BANK[t % 2]][0:ROWS[t], 0:E], h1b[0:ROWS[t], t, :],
                                        ALU.add).then_inc(res_ready, 1)


def key_block(k_bd, bank, ch, p, hg):
    rows = slice(hg * HPAD, hg * HPAD + HALF)
    return (k_bd[rows, p, ch * CHUNK:(ch + 1) * CHUNK, hg, 0:N],
            bank[QK_BANK[(4 * ch + 2 + p) % len(QK_BANK)]][rows, 0:CHUNK * N].rearrange("r (b n) -> r b n", b=CHUNK))


def token_block(bank, xnT_hi, xnT_lo, t, images):
    cols = slice(TN[t], TN[t + 1])
    src = bank[LN1_BANK[t]][0:EH, 0:2 * ROWS[t]].rearrange("r (k n b) -> r k n b", k=2, b=B)[:, :, :, images]
    return (src, *(x[:, :, images, cols].rearrange("r k b n -> r k n b") for x in (xnT_hi, xnT_lo)))


def value_block(oT, bank, u, s):
    rows = slice(2 * D * s, 2 * D * (s + 1))
    dst = oT[rows, :, :, u * UNIT:(u + 1) * UNIT].rearrange("r p n i -> r i p n")
    src = bank[PV_BANK[u % 2]][rows, 0:4 * SP].rearrange("r (i p s n) -> r i p s n", i=UNIT, p=2, s=SLOTS)[:, :, :, s, :]
    return dst, src


_INS = ['x', 'L0_tok_g1', 'L0_tok_Wp', 'L0_tok_bp', 'L0_tok_g2', 'L0_attn_w_qkv', 'L0_attn_w_out', 'L0_ffn_moe0_W1',
        'L0_ffn_moe0_b1', 'L0_ffn_moe0_W2', 'L0_ffn_moe0_b2', 'L0_ffn_A1_W', 'L0_ffn_A1_b', 'L0_ffn_A2_W',
        'L0_ffn_A2_b', 'L0_ffn_G_W']


def kernel(**inputs):
    import numpy as _np
    import concourse.bacc as _bacc
    from concourse import mybir as _mybir
    from concourse.bass_utils import run_bass_kernel_spmd as _run

    nc = _bacc.Bacc("TRN2", target_bir_lowering=False, num_devices=1)
    arrays, args = {}, []
    for name in _INS:
        a = _np.ascontiguousarray(inputs[name])
        arrays[f"in_{name}_dram"] = a
        args.append(nc.dram_tensor(f"in_{name}_dram", a.shape, _mybir.dt.from_np(a.dtype), kind="ExternalInput").ap())
    args.append(nc.dram_tensor("out_0_dram", (B, N, E), F32, kind="ExternalOutput").ap())
    vit_tower(nc, *args)
    r = _run(nc, [arrays], core_ids=[0])
    return r.results[0]["out_0_dram"]
```
